# Optimizing a Trainium2 kernel written in Bass

```python
import numpy as np
import jax
import jax.numpy as jnp

def _softmax(x, axis=-1):
    return jax.nn.softmax(x, axis=axis)

def _gelu(x):
    return jax.nn.gelu(x, approximate=True)

def _silu(x):
    return jax.nn.silu(x)

def _sigmoid(x):
    return jax.nn.sigmoid(x)

def _layernorm(x, axis=-1, eps=1e-05):
    m = jnp.mean(x, axis=axis, keepdims=True)
    v = jnp.var(x, axis=axis, keepdims=True)
    return (x - m) / jnp.sqrt(v + eps)

def _scatter_add(tgt, idx, src, axis=0):
    return tgt.at[idx].add(src)

def _segment_sum(src, seg, n):
    return jax.ops.segment_sum(src, seg, n)
kernel_name = 'mk_flamingo_gated_d1_seqx_r4_0d0f90'

def setup_inputs(seed: int=0):
    np.random.seed(seed)
    _w = jnp.asarray

    def _rec_inputs():
        import jax
        import jax.numpy as jnp
        _rk = jax.random.key(seed)
        x = -0.0002928 + 1 * jax.random.normal(jax.random.fold_in(_rk, 1), (32, 256, 256), jnp.float32)
        _lenS = 256 - jax.random.randint(jax.random.fold_in(_rk, 7), (32,), 0, max(1, 256 // 4) + 1, jnp.int32)
        _lenS2 = 256 - jax.random.randint(jax.random.fold_in(_rk, 8), (32,), 0, max(1, 256 // 4) + 1, jnp.int32)
        _ctx_1024P = jax.random.normal(jax.random.fold_in(_rk, 11), (32, 16, 256), jnp.float32)
        _ctx_1024c = jax.random.dirichlet(jax.random.fold_in(_rk, 511), 0.3 * jnp.ones((16,), jnp.float32), (32, 256))
        _ctx_1024t = jnp.einsum('bsk,bkd->bsd', _ctx_1024c, _ctx_1024P)
        _ctx_1024t = _ctx_1024t * jax.lax.rsqrt(jnp.mean(jnp.square(_ctx_1024t)) + 1e-12) * 0.953939
        ctx_1024 = -1.39393e-06 + 0.999914 * (_ctx_1024t + 0.3 * jax.random.normal(jax.random.fold_in(_rk, 611), (32, 256, 256), jnp.float32))
        _g = jax.random.normal(jax.random.fold_in(_rk, 9001), (2, 1), jnp.float32)
        _g = jnp.sign(_g) * jnp.maximum(jnp.abs(_g), 1.0) + (_g == 0) * 1.0
        g_xattn = _g[0]
        g_ffn = _g[1]
        return (x, ctx_1024, g_xattn, g_ffn)
    x, ctx_1024, g_xattn, g_ffn = _rec_inputs()

    def _L0_xattn_setup():
        import jax, jax.numpy as jnp
        import numpy as np
        B, S, D, NH = (2, 512, 256, 8)
        DH = D // NH
        EPS = 1e-06
        LN_EPS = 1e-05

        def _mlstm_cell(q, k, v, igate_w, igate_b, fgate_w, fgate_b, ln_scale):
            Slen = q.shape[0]
            ifg = jnp.concatenate([q, k, v], axis=-1)
            ig = (ifg @ igate_w.T + igate_b).T
            fg = (ifg @ fgate_w.T + fgate_b).T
            qh = q.reshape(Slen, NH, DH).transpose(1, 0, 2)
            kh = k.reshape(Slen, NH, DH).transpose(1, 0, 2)
            vh = v.reshape(Slen, NH, DH).transpose(1, 0, 2)
            log_f = jax.nn.log_sigmoid(fg)
            cs = jnp.cumsum(log_f, axis=1)
            fg_mat = cs[:, :, None] - cs[:, None, :]
            mask = jnp.tril(jnp.ones((Slen, Slen), dtype=bool))
            log_fg_mat = jnp.where(mask, fg_mat, -jnp.inf)
            log_D = log_fg_mat + ig[:, None, :]
            max_log_D = jnp.max(log_D, axis=-1, keepdims=True)
            D_mat = jnp.exp(log_D - max_log_D)
            qk = jnp.einsum('hsd,htd->hst', qh, kh) / np.sqrt(DH)
            C = qk * D_mat
            normalizer = jnp.maximum(jnp.abs(C.sum(axis=-1, keepdims=True)), jnp.exp(-max_log_D))
            h = jnp.einsum('hst,htd->hsd', C / (normalizer + EPS), vh)
            h = h.transpose(1, 0, 2).reshape(Slen, D)
            mu = h.mean(axis=-1, keepdims=True)
            var = h.var(axis=-1, keepdims=True)
            return (h - mu) / jnp.sqrt(var + LN_EPS) * ln_scale
        key = jax.random.key(seed)
        ks = jax.random.split(key, 8)
        rnd = lambda k, sh, s=1.0: jax.random.normal(k, sh, dtype=jnp.float32) * s
        return {'q': rnd(ks[0], (B, S, D)), 'k': rnd(ks[1], (B, S, D)), 'v': rnd(ks[2], (B, S, D)), 'igate_w': rnd(ks[3], (NH, 3 * D), 0.02), 'igate_b': jnp.linspace(3.0, 6.0, NH, dtype=jnp.float32), 'fgate_w': rnd(ks[4], (NH, 3 * D), 0.02), 'fgate_b': rnd(ks[5], (NH,), 0.3162278), 'ln_scale': jnp.ones((D,), dtype=jnp.float32)}
    _L0_xattn_all = _L0_xattn_setup()
    _L0_xattn_in = {k: v for k, v in _L0_xattn_all.items() if k in ('igate_w', 'igate_b', 'fgate_w', 'fgate_b', 'ln_scale')}
    del _L0_xattn_all

    def _L0_ffn_setup():
        import jax, jax.numpy as jnp
        import numpy as np
        import math
        BETA = 0.9
        THRESHOLD = 1.0
        NUM_STEPS = 5
        ALPHA = 2.0

        @jax.custom_vjp
        def spike_fn(u):
            return (u > 0).astype(u.dtype)

        def _spike_fwd(u):
            return (spike_fn(u), u)

        def _spike_bwd(u, g):
            s = jnp.pi / 2.0 * ALPHA * u
            return (g * (ALPHA / 2.0) / (1.0 + s * s),)
        spike_fn.defvjp(_spike_fwd, _spike_bwd)
        key = jax.random.key(seed)
        k1, k2, k3 = jax.random.split(key, 3)
        n_embd = 256
        x = jax.random.normal(k1, (4, 512, n_embd), dtype=jnp.float32)
        W_fc = jax.random.normal(k2, (4 * n_embd, n_embd), dtype=jnp.float32) / math.sqrt(n_embd)
        W_proj = jax.random.normal(k3, (n_embd, 4 * n_embd), dtype=jnp.float32) / math.sqrt(4 * n_embd)
        return {'x': x, 'W_fc': W_fc, 'W_proj': W_proj}
    _L0_ffn_all = _L0_ffn_setup()
    _L0_ffn_in = {k: v for k, v in _L0_ffn_all.items() if k in ('W_fc', 'W_proj')}
    del _L0_ffn_all
    return {'x': x, 'ctx_1024': ctx_1024, 'g_xattn': g_xattn, 'g_ffn': g_ffn, 'L0_xattn_igate_w': _L0_xattn_in['igate_w'], 'L0_xattn_igate_b': _L0_xattn_in['igate_b'], 'L0_xattn_fgate_w': _L0_xattn_in['fgate_w'], 'L0_xattn_fgate_b': _L0_xattn_in['fgate_b'], 'L0_xattn_ln_scale': _L0_xattn_in['ln_scale'], 'L0_ffn_W_fc': _L0_ffn_in['W_fc'], 'L0_ffn_W_proj': _L0_ffn_in['W_proj']}

def reference(x, ctx_1024, g_xattn, g_ffn, L0_xattn_igate_w, L0_xattn_igate_b, L0_xattn_fgate_w, L0_xattn_fgate_b, L0_xattn_ln_scale, L0_ffn_W_fc, L0_ffn_W_proj):
    import jax
    import jax.numpy as jnp

    def _L0_xattn_ref(q, k, v, igate_w, igate_b, fgate_w, fgate_b, ln_scale):
        import jax, jax.numpy as jnp
        import numpy as np
        B, S, D, NH = (2, 512, 256, 8)
        DH = D // NH
        EPS = 1e-06
        LN_EPS = 1e-05

        def _mlstm_cell(q, k, v, igate_w, igate_b, fgate_w, fgate_b, ln_scale):
            Slen = q.shape[0]
            ifg = jnp.concatenate([q, k, v], axis=-1)
            ig = (ifg @ igate_w.T + igate_b).T
            fg = (ifg @ fgate_w.T + fgate_b).T
            qh = q.reshape(Slen, NH, DH).transpose(1, 0, 2)
            kh = k.reshape(Slen, NH, DH).transpose(1, 0, 2)
            vh = v.reshape(Slen, NH, DH).transpose(1, 0, 2)
            log_f = jax.nn.log_sigmoid(fg)
            cs = jnp.cumsum(log_f, axis=1)
            fg_mat = cs[:, :, None] - cs[:, None, :]
            mask = jnp.tril(jnp.ones((Slen, Slen), dtype=bool))
            log_fg_mat = jnp.where(mask, fg_mat, -jnp.inf)
            log_D = log_fg_mat + ig[:, None, :]
            max_log_D = jnp.max(log_D, axis=-1, keepdims=True)
            D_mat = jnp.exp(log_D - max_log_D)
            qk = jnp.einsum('hsd,htd->hst', qh, kh) / np.sqrt(DH)
            C = qk * D_mat
            normalizer = jnp.maximum(jnp.abs(C.sum(axis=-1, keepdims=True)), jnp.exp(-max_log_D))
            h = jnp.einsum('hst,htd->hsd', C / (normalizer + EPS), vh)
            h = h.transpose(1, 0, 2).reshape(Slen, D)
            mu = h.mean(axis=-1, keepdims=True)
            var = h.var(axis=-1, keepdims=True)
            return (h - mu) / jnp.sqrt(var + LN_EPS) * ln_scale
        return jax.vmap(lambda qq, kk, vv: _mlstm_cell(qq, kk, vv, igate_w, igate_b, fgate_w, fgate_b, ln_scale))(q, k, v)

    def _L0_ffn_ref(x, W_fc, W_proj):
        import jax, jax.numpy as jnp
        import numpy as np
        import math
        BETA = 0.9
        THRESHOLD = 1.0
        NUM_STEPS = 5
        ALPHA = 2.0

        @jax.custom_vjp
        def spike_fn(u):
            return (u > 0).astype(u.dtype)

        def _spike_fwd(u):
            return (spike_fn(u), u)

        def _spike_bwd(u, g):
            s = jnp.pi / 2.0 * ALPHA * u
            return (g * (ALPHA / 2.0) / (1.0 + s * s),)
        spike_fn.defvjp(_spike_fwd, _spike_bwd)
        h = jnp.square(jax.nn.relu(jnp.einsum('bsd,fd->bsf', x, W_fc)))
        y = jnp.einsum('bsf,df->bsd', h, W_proj)

        def step(mem, _):
            reset = jax.lax.stop_gradient(spike_fn(mem - THRESHOLD))
            mem_new = BETA * mem + y - reset * THRESHOLD
            spk = spike_fn(mem_new - THRESHOLD)
            return (mem_new, spk)
        mem0 = jnp.zeros_like(y)
        _, spks = jax.lax.scan(step, mem0, None, length=NUM_STEPS)
        return jnp.sum(spks, axis=0) / NUM_STEPS
    x = x + jnp.tanh(g_xattn[0]) * _L0_xattn_ref(_layernorm(x, axis=-1), ctx_1024, ctx_1024, L0_xattn_igate_w, L0_xattn_igate_b, L0_xattn_fgate_w, L0_xattn_fgate_b, L0_xattn_ln_scale)
    x = x + jnp.tanh(g_ffn[0]) * _L0_ffn_ref(_layernorm(x, axis=-1), L0_ffn_W_fc, L0_ffn_W_proj)
    return x

_drawn_inputs = setup_inputs


def setup_inputs(seed=0):
    import zlib

    import numpy as np

    out = dict(_drawn_inputs(seed))
    spreads = {'L0_xattn_ln_scale': (1.0, 0.2)}
    factors = {}
    for name, (base, spread) in spreads.items():
        noise = np.random.default_rng([zlib.crc32(name.encode()), seed]).standard_normal(out[name].shape)
        drawn = base * np.exp(spread * noise) if base else spread * noise
        out[name] = jnp.asarray(drawn.astype(out[name].dtype))
    for name, factor in factors.items():
        out[name] = (out[name] * factor).astype(out[name].dtype)
    return out
```

```python
from contextlib import ExitStack

import numpy as np
import concourse.bass as bass
from concourse import mybir


def lif_thresholds(beta, threshold, steps, top=4.0):
    one, b, th = np.float32(1), np.float32(beta), np.float32(threshold)

    def count(y):
        mem, n = np.float32(0), 0
        for _ in range(steps):
            reset = one if mem - th > 0 else np.float32(0)
            mem = np.float32(np.float32(np.float32(b * mem) + y) - reset * th)
            n += int(mem - th > 0)
        return n

    found = []
    for n in range(1, steps + 1):
        lo, hi = np.float32(0), np.float32(top)
        while True:
            mid = np.float32((float(lo) + float(hi)) / 2)
            if mid == lo or mid == hi:
                break
            lo, hi = (lo, mid) if count(mid) >= n else (mid, hi)
        found.append(float(lo))
    return found


def build_block(nc, x, ctx_rows, ctx_cols, g_xattn, g_ffn, gate_w, gate_b, ln_scale, w_fc_t, w_proj_t, out):
    fp32, bf16, fp32r = mybir.dt.float32, mybir.dt.bfloat16, mybir.dt.float32r
    ALU, ACT = mybir.AluOpType, mybir.ActivationFunctionType

    P = 128
    B, S, D = x.shape
    NH = gate_b.shape[1]
    DH = D // NH
    F = w_fc_t.shape[1]
    ST = S // P
    DC = D // P
    HPC = P // DH
    FT = F // P
    PAIRS = B // 2
    PT = 2 * S
    BANK = 512
    VW = DH + 1
    EPS, LN_EPS = 1e-6, 1e-5
    MASKED = -1.0e30
    LOG_QK_SCALE = -0.5 * float(np.log(DH))
    THETA = lif_thresholds(0.9, 1.0, 5)
    STEPS = len(THETA)

    UNITS = [(0, (0, 1)), (0, (2, 3)), (1, (0, 1, 2, 3)), (0, (4, 5)), (0, (6, 7)), (1, (4, 5, 6, 7))]
    U = len(UNITS)
    Z_SLOTS = [0, 1, 3, 4, 6, 7, 9, 10]

    NX, NC, NQ, NST, NV, NAM, NUN, NCH, NX1, NX2, NHF, NRE = 5, 2, 2, 3, 3, 3, 3, 6, 3, 2, 2, 3

    with ExitStack() as ctx:
        def sb(name, shape, dt):
            return ctx.enter_context(nc.sbuf_tensor(name, shape, dt))

        def ps(name, shape, dt=fp32):
            return ctx.enter_context(nc.psum_tensor(name, shape, dt))

        ident = sb("ident", [P, P], fp32)
        ident_b = sb("ident_b", [P, P], bf16)
        behind = sb("behind", [P, P], bf16)
        scale_row = sb("scale_row", [P, D], fp32)
        g_col = sb("g_col", [P, 2], fp32)
        tanh_g = sb("tanh_g", [P, 2], fp32)
        rate_g = sb("rate_g", [P, 1], fp32)
        eps_col = sb("eps_col", [P, 1], fp32)
        lqk_col = sb("lqk_col", [P, 1], fp32)
        ibias = sb("ibias", [2 * NH, 1], fp32)
        fbias = sb("fbias", [2 * NH, 1], fp32)
        gw_raw = sb("gw_raw", [P, 3 * DC, 2 * NH], fp32)
        gw_sum = sb("gw_sum", [P, 2 * DC, 2 * NH], fp32)
        gw_hi = sb("gw_hi", [P, 2 * DC, 2 * NH], bf16)
        gw_lo = sb("gw_lo", [P, 2 * DC, 2 * NH], bf16)
        w_raw = sb("w_raw", [P, DC * F], fp32)
        wfc_hi = sb("wfc_hi", [P, DC, F], fp32r)
        wfc_lo = sb("wfc_lo", [P, DC, F], fp32r)
        wpr_hi = sb("wpr_hi", [P, FT, D], fp32r)
        wpr_lo = sb("wpr_lo", [P, FT, D], fp32r)

        x_in = [sb(f"x_in{i}", [P, ST, D], fp32) for i in range(NX)]
        v_in = [sb(f"v_in{i}", [P, ST, D], fp32) for i in range(NC)]
        kT_in = [sb(f"kT_in{i}", [P, DC, S], fp32) for i in range(NC)]
        stat1 = sb("stat1", [P, ST, 6], fp32)
        mv1 = [sb(f"mv1_{i}", [P, ST, 2], fp32) for i in range(2)]
        rstd1 = [sb(f"rstd1_{i}", [P, ST], fp32) for i in range(2)]
        lnv1 = sb("lnv1", [P, ST], fp32)
        xln = sb("xln", [P, ST, D], fp32)
        qT_hi = [sb(f"qT_hi{i}", [P, DC, S], bf16) for i in range(NQ)]
        qT_lo = [sb(f"qT_lo{i}", [P, DC, S], bf16) for i in range(NQ)]
        kT_hi = [sb(f"kT_hi{i}", [P, DC, S], bf16) for i in range(NQ)]
        kT_lo = [sb(f"kT_lo{i}", [P, DC, S], bf16) for i in range(NQ)]
        q_stack = [sb(f"q_stack{i}", [P, NH, S], bf16) for i in range(NST)]
        k_stack = [sb(f"k_stack{i}", [P, NH, S], bf16) for i in range(NST)]
        v_hi = [sb(f"v_hi{i}", [P, ST, NH, VW], bf16) for i in range(NV)]
        v_lo = [sb(f"v_lo{i}", [P, ST, NH, DH], bf16) for i in range(NV)]

        R = 2 * NH
        gates = [sb(f"gates{i}", [P, 2, ST, R], fp32) for i in range(2)]
        f_neg = sb("f_neg", [R, S], fp32)
        i_pre = sb("i_pre", [R, S], fp32)
        f_log = sb("f_log", [R, S], fp32)
        cs = sb("cs", [R, S], fp32)
        am = sb("am", [R, 2, S], fp32)
        row_max = sb("row_max", [R, S], fp32)
        am_rest = sb("am_rest", [R, 2, S], fp32)
        am_part = sb("am_part", [R, 3, 2, S], bf16)
        a_rows = [sb(f"a_rows{i}", [P, NH, S], bf16) for i in range(NAM)]
        m_rows = [sb(f"m_rows{i}", [P, NH, S], bf16) for i in range(NAM)]
        floor = [sb(f"floor{i}", [P, ST, R], fp32) for i in range(3)]

        decay = [sb(f"decay{i}", [P, BANK], fp32) for i in range(NUN)]
        c_hi = [sb(f"c_hi{i}", [P, BANK], bf16) for i in range(NCH)]
        c_lo = [sb(f"c_lo{i}", [P, BANK], bf16) for i in range(NCH)]

        denom = sb("denom", [P, ST, NH], fp32)
        rdenom = sb("rdenom", [P, ST, NH], fp32)
        h_rows = sb("h_rows", [P, ST, D], fp32)
        stat2 = sb("stat2", [P, ST, 6], fp32)
        mv2 = sb("mv2", [P, ST, 2], fp32)
        lnv2 = sb("lnv2", [P, ST], fp32)
        rstd2 = sb("rstd2", [P, ST], fp32)
        rstd2g = sb("rstd2g", [P, ST], fp32)
        x1 = [sb(f"x1_{i}", [P, 2 * ST, D], fp32) for i in range(NX1)]
        stat3 = sb("stat3", [P, ST, 6], fp32)
        mv3 = sb("mv3", [P, ST, 2], fp32)
        lnv3 = sb("lnv3", [P, ST], fp32)
        rstd3 = sb("rstd3", [P, ST], fp32)
        x1ln = sb("x1ln", [P, ST, D], fp32)
        x2_hi = [sb(f"x2_hi{i}", [P, DC, PT], fp32r) for i in range(NX2)]
        x2_lo = [sb(f"x2_lo{i}", [P, DC, PT], fp32r) for i in range(NX2)]

        relu = [sb(f"relu{i}", [P, PT], fp32) for i in range(NRE)]
        h_hi = [sb(f"h_hi{i}", [P, PT], fp32r) for i in range(NHF)]
        h_lo = [sb(f"h_lo{i}", [P, PT], fp32r) for i in range(NHF)]
        y_sb = w_raw[:, 0:DC * PT].rearrange("p (c s) -> p c s", c=DC)
        spikes = sb("spikes", [P, DC, PT], bf16)
        out_sb = w_raw[:, DC * PT:2 * DC * PT].rearrange("p (t d) -> p t d", d=D)

        arg_ps = ps("arg_ps", [P, BANK])
        qk_ps = ps("qk_ps", [P, BANK])
        z_ps = ps("z_ps", [P, BANK])
        misc_ps = ps("misc_ps", [P, BANK])
        pv_ps = ps("pv_ps", [P, ST, BANK])
        y_ps = ps("y_ps", [P, DC, BANK])
        misc_spikes = misc_ps[:, :].bitcast(bf16).rearrange("p (t d) -> p t d", d=D)
        pv_heads = pv_ps[:, :, 0:NH * VW].rearrange("p t (h c) -> p t h c", c=VW)

        sems = {}

        def sem(name):
            if name not in sems:
                sems[name] = ctx.enter_context(nc.semaphore(name))
            return sems[name]

        def after(eng, stage, n):
            if n >= 0:
                eng.wait_ge(sem(stage), n + 1)

        def landed(eng, ring, slot, n, dmas):
            eng.wait_ge(sem(f"{ring}{slot}"), 16 * dmas * (n + 1))

        streams = {k: [] for k in ("sync", "scalar", "vector", "tensor", "gpsimd")}

        def at(engine, time, step, *args):
            streams[engine].append((time, len(streams[engine]), step, args))

        def play(engine, eng):
            for _, _, step, args in sorted(streams[engine], key=lambda e: e[:2]):
                step(eng, *args)

        chains = {}

        def link(eng, which, ins):
            chains[which] = chains.get(which, 0) + 1
            ins.then_inc(sem(f"chain_{which}"), 1)
            eng.wait_ge(sem(f"chain_{which}"), chains[which])

        misc_users = []

        def misc_turn(eng, user):
            order = sorted(misc_users)
            after(eng, "misc_free", [u for _, u in order].index(user) - 1)

        def setup_loads(e):
            e.dma_start(w_raw[:, :], w_fc_t.rearrange("(c p) f -> p c f", p=P)).then_inc(sem("ld_wfc"), 16)
            e.dma_start(gw_raw[:, :, :], gate_w.rearrange("(c p) g -> p c g", p=P)).then_inc(sem("ld_small"), 16)
            e.dma_start(scale_row[:, :], ln_scale.partition_broadcast(P)).then_inc(sem("ld_small"), 16)
            e.dma_start(g_col[:, 0:1], g_xattn.partition_broadcast(P)).then_inc(sem("ld_small"), 16)
            e.dma_start(g_col[:, 1:2], g_ffn.partition_broadcast(P)).then_inc(sem("ld_small"), 16)
            for b in range(2):
                for row, col in enumerate((ibias, fbias)):
                    e.dma_start(col[b * NH:(b + 1) * NH, :], gate_b[row, :].unsqueeze(1)).then_inc(sem("ld_small"), 16)
        SMALL_LOADS = 8 * 16

        def setup_load_wproj(e):
            after(e, "wfc_ready", 0)
            e.dma_start(w_raw[:, :], w_proj_t.rearrange("(j p) d -> p j d", p=P)).then_inc(sem("ld_wpr"), 16)

        def setup_pool(e):
            e.memset(ident[:, :], 0.0).then_inc(sem("zeroed"), 1)
            e.memset(ident_b[:, :], 0.0).then_inc(sem("zeroed"), 1)
            e.memset(behind[:, :], 0.0).then_inc(sem("zeroed"), 1)
            for t in v_hi:
                last = e.memset(t[:, :, :, DH:VW], 1.0)
            last.then_inc(sem("zeroed"), 1)
            e.wait_ge(sem("zeroed"), 4)
            e.affine_select(out=behind[:, :], in_=behind[:, :], compare_op=ALU.is_ge, fill=MASKED, base=0,
                            pattern=[[1, P]], channel_multiplier=-1).then_inc(sem("ident_ready"), 1)
            for t in (ident, ident_b):
                e.affine_select(out=t[:, :], in_=t[:, :], compare_op=ALU.not_equal, fill=1.0, base=0,
                                pattern=[[-1, P]], channel_multiplier=1).then_inc(sem("ident_ready"), 1)

        def setup_vector(e):
            e.memset(eps_col[:, :], LN_EPS)
            e.memset(lqk_col[:, :], LOG_QK_SCALE).then_inc(sem("cols_ready"), 1)
            for t in m_rows:
                link(e, "vector", e.memset(t[:, :, :], 0.0))
                e.memset(t[0:3, :, :], 1.0)
            for t in a_rows:
                last = e.memset(t[:, :, :], -1.0)
            last.then_inc(sem("rows_ready"), 1)
            e.wait_ge(sem("ld_small"), SMALL_LOADS)
            e.tensor_copy(gw_sum[:, 0:DC, :], gw_raw[:, 0:DC, :])
            link(e, "vector", e.tensor_tensor(gw_sum[:, DC:, :], gw_raw[:, DC:2 * DC, :], gw_raw[:, 2 * DC:, :], ALU.add))
            link(e, "vector", e.tensor_copy(gw_hi[:, :, :], gw_sum[:, :, :]))
            e.tensor_tensor(gw_lo[:, :, :], gw_sum[:, :, :], gw_hi[:, :, :], ALU.subtract).then_inc(sem("gw_ready"), 1)
            after(e, "tanh_ready", 0)
            e.tensor_scalar(rate_g[:, :], tanh_g[:, 1:2], 1.0 / STEPS, None, ALU.mult)

        def split_weights(e, stage, load, hi, lo):
            e.wait_ge(sem(load), 16)
            flat = "p a b -> p (a b)"
            link(e, "vector", e.tensor_copy(hi[:, :, :].rearrange(flat), w_raw[:, :]))
            e.tensor_tensor(lo[:, :, :].rearrange(flat), w_raw[:, :], hi[:, :, :].bitcast(fp32).rearrange(flat),
                            ALU.subtract).then_inc(sem(stage), 1)

        def setup_tanh(e):
            e.wait_ge(sem("ld_small"), SMALL_LOADS)
            e.activation(tanh_g[:, :], g_col[:, :], ACT.Tanh).then_inc(sem("tanh_ready"), 1)

        def load_batch(e, b):
            after(e, "x1_done", b - NX)
            e.dma_start(x_in[b % NX][:, :, :], x[b].rearrange("(t p) d -> p t d", p=P)).then_inc(sem(f"ld_x{b % NX}"), 16)
            after(e, "k_split", b - NC)
            e.dma_start(kT_in[b % NC][:, :, :], ctx_cols[b].rearrange("(c p) s -> p c s", p=P)).then_inc(sem(f"ld_k{b % NC}"), 16)

        def load_values(e, b):
            after(e, "v_split", b - NC)
            e.dma_start(v_in[b % NC][:, :, :], ctx_rows[b].rearrange("(t p) d -> p t d", p=P)).then_inc(sem(f"ld_v{b % NC}"), 16)

        def row_stats(e, src, stat, mv):
            for t in range(ST):
                ins = e.bn_stats(stat[:, t, :], src[:, t, :])
            link(e, "vector", ins)
            for t in range(ST):
                ins = e.bn_aggr(mv[:, t, :], stat[:, t, :])
            return ins

        def rstd_of(e, rstd, lnv, mv):
            link(e, "scalar", e.activation(lnv[:, :], mv[:, :, 1], ACT.Ln, bias=eps_col[:, :]))
            return e.activation(rstd[:, :], lnv[:, :], ACT.Exp, scale=-0.5)

        def normalise(e, dst, src, mv, rstd):
            for t in range(ST):
                ins = e.tensor_scalar(dst[:, t, :], src[:, t, :], mv[:, t, 0:1], rstd[:, t:t + 1], ALU.subtract, ALU.mult)
            return ins

        def ln1_stats(e, b):
            landed(e, "ld_x", b % NX, b // NX, 1)
            after(e, "xln", b - 2)
            row_stats(e, x_in[b % NX], stat1, mv1[b % 2]).then_inc(sem("ln1_stats"), 1)

        def ln1_rstd(e, b):
            after(e, "cols_ready", 0)
            after(e, "ln1_stats", b)
            after(e, "xln", b - 2)
            rstd_of(e, rstd1[b % 2], lnv1, mv1[b % 2]).then_inc(sem("ln1_rstd"), 1)

        def ln1_apply(e, b):
            after(e, "ln1_rstd", b)
            after(e, "q_T", b - 1)
            normalise(e, xln, x_in[b % NX], mv1[b % 2], rstd1[b % 2]).then_inc(sem("xln"), 1)

        def k_split(e, b):
            landed(e, "ld_k", b % NC, b // NC, 1)
            after(e, "gates", b - NQ)
            if b >= NQ:
                landed(e, "ld_stack", (b - NQ) % NST, (b - NQ) // NST, STACK_DMAS)
            src, hi, lo = kT_in[b % NC], kT_hi[b % NQ], kT_lo[b % NQ]
            link(e, "gpsimd", e.tensor_copy(hi[:, :, :], src[:, :, :]))
            e.tensor_tensor(lo[:, :, :], src[:, :, :], hi[:, :, :], ALU.subtract).then_inc(sem("k_split"), 1)

        def v_split(e, b):
            landed(e, "ld_v", b % NC, b // NC, 1)
            after(e, "pv", 2 * (b - NV) + 1)
            src = v_in[b % NC][:, :, :].rearrange("p t (h d) -> p t h d", d=DH)
            hi, lo = v_hi[b % NV][:, :, :, 0:DH], v_lo[b % NV]
            link(e, "gpsimd", e.tensor_copy(hi, src))
            e.tensor_tensor(lo[:, :, :, :], src, hi, ALU.subtract).then_inc(sem("v_split"), 1)

        def transpose_rows(e, src):
            for c in range(DC):
                for t in range(ST):
                    col = c * S + t * P
                    ins = e.transpose(misc_ps[:, col:col + P], src[:, t, c * P:(c + 1) * P], ident[:, :])
            return ins

        def q_T(e, b):
            e.wait_ge(sem("ident_ready"), 3)
            after(e, "xln", b)
            misc_turn(e, ("q", b))
            transpose_rows(e, xln).then_inc(sem("q_T"), 1)

        def misc_chunks():
            return misc_ps[:, :].rearrange("p (c s) -> p c s", c=DC)

        def q_hi(e, b):
            after(e, "q_T", b)
            after(e, "gates", b - NQ)
            if b >= NQ:
                landed(e, "ld_stack", (b - NQ) % NST, (b - NQ) // NST, STACK_DMAS)
            e.activation(qT_hi[b % NQ][:, :, :], misc_chunks(), ACT.Copy).then_inc(sem("q_hi"), 1)

        def q_lo(e, b):
            after(e, "q_hi", b)
            e.tensor_tensor(qT_lo[b % NQ][:, :, :], misc_chunks(), qT_hi[b % NQ][:, :, :],
                            ALU.subtract).then_inc(sem("misc_free"), 1)

        def misc_use(user):
            return [u for _, u in sorted(misc_users)].index(user)

        STACK_Q = ((0, qT_hi), (2, qT_hi), (1, qT_lo), (3, qT_lo))
        STACK_K = ((0, kT_hi), (1, kT_hi), (2, kT_lo), (3, kT_lo))
        STACK_DMAS = HPC * (len(STACK_Q) + len(STACK_K))

        def stack_heads(e, b):
            slot = b % NST
            done = sem(f"ld_stack{slot}")
            after(e, "k_split", b)
            after(e, "misc_free", misc_use(("q", b)))
            after(e, "cmul", U * (b - NST) + U - 1)
            for stack, parts in ((k_stack, STACK_K), (q_stack, STACK_Q)):
                for j, part in parts:
                    for g in range(HPC):
                        dst = stack[slot][DH * j:DH * (j + 1), :, :].rearrange("d (c g) s -> d c g s", g=HPC)[:, :, g, :]
                        e.dma_start(dst, part[b % NQ][DH * g:DH * (g + 1), :, :]).then_inc(done, 16)

        def gate_products(e, b):
            after(e, "gw_ready", 0)
            after(e, "k_split", b)
            after(e, "misc_free", misc_use(("q", b)))
            misc_turn(e, ("g", b))
            n = b % NQ
            for t in range(ST):
                terms = [(part[n][:, c, t * P:(t + 1) * P], w[:, k * DC + c, :])
                         for k, (hi, lo) in enumerate(((qT_hi, qT_lo), (kT_hi, kT_lo)))
                         for c in range(DC)
                         for part, w in ((hi, gw_hi), (hi, gw_lo), (lo, gw_hi))]
                for i, (lhsT, rhs) in enumerate(terms):
                    ins = e.matmul(misc_ps[:, t * R:(t + 1) * R], lhsT, rhs, start=(i == 0), stop=(i == len(terms) - 1))
            ins.then_inc(sem("gates"), 1)

        def gates_out(e, b):
            after(e, "gates", b)
            after(e, "gate_T", b // 2 - 2)
            src = misc_ps[:, 0:ST * R].rearrange("p (t k h) -> p k t h", t=ST, k=2)
            e.activation(gates[b // 2 % 2][:, :, :, b % 2 * NH:(b % 2 + 1) * NH], src, ACT.Copy).then_inc(sem("misc_free"), 1)

        def gate_T(e, p):
            after(e, "misc_free", misc_use(("g", 2 * p + 1)))
            misc_turn(e, ("gT", p))
            for k in range(2):
                for t in range(ST):
                    col = k * S + t * P
                    ins = e.transpose(misc_ps[0:R, col:col + P], gates[p % 2][:, k, t, :], ident[:, :])
            ins.then_inc(sem("gate_T"), 1)

        def gate_softplus(e, p):
            after(e, "gate_T", p)
            after(e, "gate_scan", p - 1)
            ins = e.activation(f_log[:, :], misc_ps[0:R, S:2 * S], ACT.Abs, bias=fbias[:, :])
            ins.then_inc(sem("gate_abs"), 1)
            after(e, "gate_abs", p)
            link(e, "scalar", e.activation(f_log[:, :], f_log[:, :], ACT.Exp, scale=-1.0))
            e.activation(f_log[:, :], f_log[:, :], ACT.Ln, bias=1.0).then_inc(sem("gate_softplus"), 1)

        def gate_pre(e, p):
            after(e, "gate_abs", p)
            e.tensor_scalar(f_neg[:, :], misc_ps[0:R, S:2 * S], fbias[:, :], 0.0, ALU.add, ALU.min)
            e.tensor_scalar(i_pre[:, :], misc_ps[0:R, 0:S], ibias[:, :], None, ALU.add).then_inc(sem("misc_free"), 1)

        def gate_scan(e, p):
            after(e, "gate_softplus", p)
            after(e, "misc_free", misc_use(("gT", p)))
            after(e, "am_split", p - 1)
            after(e, "floor_T", p - 1)
            a, m = am[:, 0, :], am[:, 1, :]
            link(e, "vector", e.tensor_tensor_scan(cs[:, :], f_neg[:, :], f_log[:, :], 0.0, ALU.add, ALU.subtract))
            link(e, "vector", e.tensor_tensor(a, i_pre[:, :], cs[:, :], ALU.subtract))
            link(e, "vector", e.tensor_tensor_scan(m, a, a, -3.0e38, ALU.max, ALU.max))
            e.tensor_tensor(row_max[:, :], m, cs[:, :], ALU.add).then_inc(sem("gate_scan"), 1)

        def am_split(e, p):
            after(e, "gate_scan", p)
            for b in (2 * p - 2, 2 * p - 1):
                if b >= 0:
                    landed(e, "ld_am", b % NAM, b // NAM, AM_DMAS)
            src, part = am, am_part
            link(e, "gpsimd", e.tensor_copy(part[:, 0, :, :], src[:, :, :]))
            link(e, "gpsimd", e.tensor_tensor(am_rest[:, :, :], src[:, :, :], part[:, 0, :, :], ALU.subtract))
            link(e, "gpsimd", e.tensor_copy(part[:, 1, :, :], am_rest[:, :, :]))
            e.tensor_tensor(part[:, 2, :, :], am_rest[:, :, :], part[:, 1, :, :], ALU.subtract).then_inc(sem("am_split"), 1)

        AM_DMAS = 6

        def am_rows(e, b):
            after(e, "rows_ready", 0)
            after(e, "am_split", b // 2)
            after(e, "arg", U * (b - NAM + 1) - 1)
            mine = slice(b % 2 * NH, (b % 2 + 1) * NH)
            for k, (rows, first) in enumerate(((a_rows, 0), (m_rows, 3))):
                for j in range(3):
                    e.dma_start(rows[b % NAM][first + j:first + j + 1, :, :], am_part[mine, j, k, :])\
                     .then_inc(sem(f"ld_am{b % NAM}"), 16)

        def floor_T(e, p):
            after(e, "gate_scan", p)
            misc_turn(e, ("fT", p))
            for t in range(ST):
                ins = e.transpose(misc_ps[:, t * R:(t + 1) * R], row_max[:, t * P:(t + 1) * P], ident[0:R, 0:R])
            ins.then_inc(sem("floor_T"), 1)

        def floor_exp(e, p):
            after(e, "floor_T", p)
            after(e, "h_norm", 2 * (p - 3) + 1)
            e.activation(floor[p % 3][:, :, :], misc_ps[:, 0:ST * R].rearrange("p (t r) -> p t r", t=ST), ACT.Exp,
                         scale=-1.0).then_inc(sem("misc_free"), 1)

        def unit_spans(kt, heads):
            n = S - kt * P
            return [(h, slice(i * n, (i + 1) * n), kt * P) for i, h in enumerate(heads)]

        def arg(e, b, u):
            kt, heads = UNITS[u]
            landed(e, "ld_am", b % NAM, b // NAM, AM_DMAS)
            after(e, "decay", b * U + u - 1)
            for h, cols, s0 in unit_spans(kt, heads):
                e.matmul(arg_ps[:, cols], a_rows[b % NAM][:, h, kt * P:(kt + 1) * P], m_rows[b % NAM][:, h, s0:S],
                         start=True, stop=False)
                ins = e.matmul(arg_ps[:, cols.start:cols.start + P], ident_b[:, :], behind[:, :], start=False, stop=True)
            ins.then_inc(sem("arg"), 1)

        def qk(e, b, u):
            kt, heads = UNITS[u]
            slot = b % NST
            landed(e, "ld_stack", slot, b // NST, STACK_DMAS)
            after(e, "cmul", b * U + u - 1)
            for h, cols, s0 in unit_spans(kt, heads):
                ins = e.matmul(qk_ps[:, cols], k_stack[slot][:, h, kt * P:(kt + 1) * P], q_stack[slot][:, h, s0:S],
                               start=True, stop=True)
            ins.then_inc(sem("qk"), 1)

        def decay_exp(e, b, u):
            i = b * U + u
            after(e, "arg", i)
            after(e, "c_lo", i - NUN)
            e.activation(decay[i % NUN][:, :], arg_ps[:, :], ACT.Exp, bias=lqk_col[:, :]).then_inc(sem("decay"), 1)

        def cmul(e, b, u):
            i = b * U + u
            after(e, "qk", i)
            after(e, "decay", i)
            e.tensor_tensor(decay[i % NUN][:, :], qk_ps[:, :], decay[i % NUN][:, :], ALU.mult).then_inc(sem("cmul"), 1)

        def c_hi_step(e, b, u):
            i = b * U + u
            after(e, "cmul", i)
            after(e, "pv", (i - NCH) // 3)
            e.activation(c_hi[i % NCH][:, :], decay[i % NUN][:, :], ACT.Copy).then_inc(sem("c_hi"), 1)

        def c_lo_step(e, b, u):
            i = b * U + u
            after(e, "c_hi", i)
            e.tensor_tensor(c_lo[i % NCH][:, :], decay[i % NUN][:, :], c_hi[i % NCH][:, :], ALU.subtract).then_inc(sem("c_lo"), 1)

        def pv(e, b, half):
            first = half * 3
            after(e, "c_lo", b * U + first + 2)
            after(e, "v_split", b)
            if half == 0:
                after(e, "h_norm", b - 1)
            for qt in range(ST):
                for h in range(half * NH // 2, (half + 1) * NH // 2):
                    blocks = []
                    for u in range(first, first + 3):
                        kt, heads = UNITS[u]
                        if h in heads and kt <= qt:
                            col = heads.index(h) * (S - kt * P) + (qt - kt) * P
                            blocks.append((kt, (b * U + u) % NCH, col))
                    out_cols = pv_ps[:, qt, h * VW:(h + 1) * VW]
                    for n, (kt, slot, col) in enumerate(blocks):
                        hi, lo = c_hi[slot][:, col:col + P], c_lo[slot][:, col:col + P]
                        vh, vl = v_hi[b % NV][:, kt, h, :], v_lo[b % NV][:, kt, h, :]
                        e.matmul(out_cols, hi, vh, start=(n == 0), stop=False, skip_group_check=True)
                        e.matmul(pv_ps[:, qt, h * VW:h * VW + DH], hi, vl, start=False, stop=False, skip_group_check=True)
                        ins = e.matmul(out_cols, lo, vh, start=False, stop=(n == len(blocks) - 1), skip_group_check=True)
            ins.then_inc(sem("pv"), 1)

        def h_norm(e, b):
            p = b // 2
            after(e, "pv", 2 * b + 1)
            after(e, "misc_free", misc_use(("fT", p)))
            row_sum, least = pv_heads[:, :, :, DH], floor[p % 3][:, :, b % 2 * NH:(b % 2 + 1) * NH]
            link(e, "vector", e.scalar_tensor_tensor(denom[:, :, :], row_sum, -1.0, least, ALU.mult, ALU.max))
            link(e, "vector", e.tensor_tensor(denom[:, :, :], denom[:, :, :], row_sum, ALU.max))
            link(e, "vector", e.tensor_scalar(denom[:, :, :], denom[:, :, :], EPS, None, ALU.add))
            link(e, "vector", e.reciprocal(rdenom[:, :, :], denom[:, :, :]))
            heads = h_rows[:, :, :].rearrange("p t (h d) -> p t h d", d=DH)
            ins = e.tensor_tensor(heads, pv_heads[:, :, :, 0:DH],
                                  rdenom[:, :, :].unsqueeze(3).broadcast_to([P, ST, NH, DH]), ALU.mult)
            ins.then_inc(sem("h_norm"), 1)
            after(e, "h_norm", b)
            row_stats(e, h_rows, stat2, mv2).then_inc(sem("ln2_stats"), 1)

        def ln2_rstd(e, b):
            after(e, "ln2_stats", b)
            after(e, "x1_done", b - 1)
            rstd_of(e, rstd2, lnv2, mv2).then_inc(sem("ln2_rstd"), 1)

        def x1_step(e, b):
            after(e, "tanh_ready", 0)
            after(e, "ln2_rstd", b)
            after(e, "out_step", b // 2 - NX1)
            for t in range(ST):
                e.scalar_tensor_tensor(h_rows[:, t, :], h_rows[:, t, :], mv2[:, t, 0:1], scale_row[:, :],
                                       ALU.subtract, ALU.mult)
            link(e, "vector", e.tensor_scalar(rstd2g[:, :], rstd2[:, :], tanh_g[:, 0:1], None, ALU.mult))
            dst = x1[b // 2 % NX1][:, b % 2 * ST:(b % 2 + 1) * ST, :]
            for t in range(ST):
                ins = e.scalar_tensor_tensor(dst[:, t, :], h_rows[:, t, :], rstd2g[:, t:t + 1], x_in[b % NX][:, t, :],
                                             ALU.mult, ALU.add)
            ins.then_inc(sem("x1_done"), 1)
            after(e, "x1_done", b)
            row_stats(e, dst, stat3, mv3).then_inc(sem("ln3_stats"), 1)

        def ln3_rstd(e, b):
            after(e, "ln3_stats", b)
            after(e, "x1ln", b - 1)
            rstd_of(e, rstd3, lnv3, mv3).then_inc(sem("ln3_rstd"), 1)

        def ln3_apply(e, b):
            after(e, "ln3_rstd", b)
            after(e, "x2_T", b - 1)
            normalise(e, x1ln, x1[b // 2 % NX1][:, b % 2 * ST:(b % 2 + 1) * ST, :], mv3, rstd3).then_inc(sem("x1ln"), 1)

        def x2_T(e, b):
            after(e, "x1ln", b)
            misc_turn(e, ("x2", b))
            transpose_rows(e, x1ln).then_inc(sem("x2_T"), 1)

        def x2_cols(tiles, b):
            return tiles[b // 2 % NX2][:, :, b % 2 * S:(b % 2 + 1) * S]

        def x2_hi_step(e, b):
            after(e, "x2_T", b)
            after(e, "z", FT * (b // 2 - NX2 + 1) - 1)
            e.activation(x2_cols(x2_hi, b), misc_chunks(), ACT.Copy).then_inc(sem("x2_hi"), 1)

        def x2_lo_step(e, b):
            after(e, "x2_hi", b)
            e.tensor_tensor(x2_cols(x2_lo, b), misc_chunks(), x2_cols(x2_hi, b).bitcast(fp32),
                            ALU.subtract).then_inc(sem("misc_free"), 1)

        def z_step(e, p, j):
            if j == 0:
                after(e, "wfc_ready", 0)
                after(e, "misc_free", misc_use(("x2", 2 * p + 1)))
            after(e, "h_full", FT * p + j - 1)
            xh, xl = x2_hi[p % NX2], x2_lo[p % NX2]
            terms = [(w[:, c, j * P:(j + 1) * P], xx[:, c, :]) for c in range(DC)
                     for w, xx in ((wfc_hi, xh), (wfc_hi, xl), (wfc_lo, xh))]
            for n, (lhsT, rhs) in enumerate(terms):
                ins = e.matmul(z_ps[:, :], lhsT, rhs, start=(n == 0), stop=(n == len(terms) - 1))
            ins.then_inc(sem("z"), 1)

        def relu_step(e, p, j):
            n = FT * p + j
            after(e, "z", n)
            after(e, "h_lo", n - NRE)
            e.activation(relu[n % NRE][:, :], z_ps[:, :], ACT.Relu).then_inc(sem("relu"), 1)

        def h_full_step(e, p, j):
            n = FT * p + j
            after(e, "relu", n)
            e.tensor_tensor(relu[n % NRE][:, :], z_ps[:, :], relu[n % NRE][:, :], ALU.mult).then_inc(sem("h_full"), 1)

        def h_hi_step(e, p, j):
            n = FT * p + j
            after(e, "h_full", n)
            after(e, "y", n - NHF)
            e.activation(h_hi[n % NHF][:, :], relu[n % NRE][:, :], ACT.Copy).then_inc(sem("h_hi"), 1)

        def h_lo_step(e, p, j):
            n = FT * p + j
            after(e, "h_hi", n)
            e.tensor_tensor(h_lo[n % NHF][:, :], relu[n % NRE][:, :], h_hi[n % NHF][:, :].bitcast(fp32),
                            ALU.subtract).then_inc(sem("h_lo"), 1)

        def y_step(e, p, j):
            n = FT * p + j
            if j == 0:
                after(e, "wpr_ready", 0)
                after(e, "y_out", p - 1)
            after(e, "h_lo", n)
            hh, hl = h_hi[n % NHF], h_lo[n % NHF]
            for c in range(DC):
                terms = [(w[:, j, c * P:(c + 1) * P], h[:, :]) for w, h in ((wpr_hi, hh), (wpr_hi, hl), (wpr_lo, hh))]
                for i, (lhsT, rhs) in enumerate(terms):
                    ins = e.matmul(y_ps[:, c, :], lhsT, rhs, start=(j == 0 and i == 0),
                                   stop=(j == FT - 1 and i == len(terms) - 1))
            ins.then_inc(sem("y"), 1)

        def y_out(e, p):
            after(e, "y", FT * p + FT - 1)
            after(e, "spikes", p - 1)
            e.activation(y_sb[:, :, :], y_ps[:, :, :], ACT.Copy).then_inc(sem("y_out"), 1)

        def spikes_step(e, p):
            after(e, "y_out", p)
            after(e, "spikes_T", p - 1)
            link(e, "vector", e.tensor_scalar(spikes[:, :, :], y_sb[:, :, :], THETA[0], None, ALU.is_gt))
            for n, theta in enumerate(THETA[1:]):
                ins = e.scalar_tensor_tensor(spikes[:, :, :], y_sb[:, :, :], theta, spikes[:, :, :], ALU.is_gt, ALU.add)
                if n < STEPS - 2:
                    link(e, "vector", ins)
            ins.then_inc(sem("spikes"), 1)

        def spikes_T(e, p):
            after(e, "spikes", p)
            misc_turn(e, ("s", p))
            for t in range(2 * ST):
                for c in range(DC):
                    ins = e.transpose(misc_spikes[:, t, c * P:(c + 1) * P], spikes[:, c, t * P:(t + 1) * P], ident_b[:, :])
            ins.then_inc(sem("spikes_T"), 1)

        def out_step(e, p):
            after(e, "spikes_T", p)
            if p >= 1:
                landed(e, "stored", 0, p - 1, 2)
            e.scalar_tensor_tensor(out_sb[:, :, :], misc_spikes, rate_g[:, :], x1[p % NX1][:, :, :], ALU.mult, ALU.add)\
             .then_inc(sem("misc_free"), 1)

        def out_mark(e, p):
            after(e, "misc_free", misc_use(("s", p)))
            e.sem_inc(sem("out_step"), 1)

        def store(e, p):
            after(e, "misc_free", misc_use(("s", p)))
            for b in range(2):
                e.dma_start(out[2 * p + b].rearrange("(t p) d -> p t d", p=P), out_sb[:, b * ST:(b + 1) * ST, :])\
                 .then_inc(sem("stored0"), 16)

        at("sync", -1e3, setup_loads)
        at("gpsimd", -1e3, setup_pool)
        at("vector", -1e3, setup_vector)
        at("vector", -21, split_weights, "wfc_ready", "ld_wfc", wfc_hi, wfc_lo)
        at("vector", -5, split_weights, "wpr_ready", "ld_wpr", wpr_hi, wpr_lo)
        at("scalar", -1e3, setup_tanh)
        at("sync", -12.5, setup_load_wproj)

        def use_misc(time, step, user, *args):
            misc_users.append((time, user))
            at("tensor", time, step, *args)

        for b in range(B):
            t0 = U * b
            f = t0 - 16
            at("sync", f - 2.5, load_batch, b)
            at("vector", f, ln1_stats, b)
            at("scalar", f + .3, ln1_rstd, b)
            at("vector", f + .8, ln1_apply, b)
            at("gpsimd", f, k_split, b)
            at("sync", t0 - 12.5, load_values, b)
            at("gpsimd", t0 - 7, v_split, b)
            use_misc(f + 1.5, q_T, ("q", b), b)
            at("scalar", f + 1.8, q_hi, b)
            at("vector", f + 2.1, q_lo, b)
            at("sync", t0 - 7.5, stack_heads, b)
            at("sync", U * (b // 2) * 2 - 3.5 if b % 2 == 0 else t0 - 6, am_rows, b)
            use_misc(f + 3, gate_products, ("g", b), b)
            at("scalar", f + 3.3, gates_out, b)
            for u in range(U):
                t = t0 + u
                at("tensor", t, arg, b, u)
                at("tensor", t + .05, qk, b, u)
                at("scalar", t + .25, decay_exp, b, u)
                at("vector", t + .7, cmul, b, u)
                at("scalar", t + 1.2, c_hi_step, b, u)
                at("gpsimd", t + 1.5, c_lo_step, b, u)
            for half in range(2):
                at("tensor", t0 + 3 * half + 4.6, pv, b, half)
            e = t0 + 8
            at("vector", e, h_norm, b)
            at("scalar", e + .3, ln2_rstd, b)
            at("vector", e + .75, x1_step, b)
            at("scalar", e + 1.0, ln3_rstd, b)
            at("vector", e + 1.4, ln3_apply, b)
            use_misc(e + 1.9, x2_T, ("x2", b), b)
            at("scalar", e + 2.2, x2_hi_step, b)
            at("vector", e + 2.5, x2_lo_step, b)
        for p in range(PAIRS):
            c = 2 * U * p - 6
            use_misc(c, gate_T, ("gT", p), p)
            at("scalar", c + .3, gate_softplus, p)
            at("vector", c + .6, gate_pre, p)
            at("vector", c + 1, gate_scan, p)
            at("gpsimd", c + 1.7, am_split, p)
            use_misc(c + 1.9, floor_T, ("fT", p), p)
            at("scalar", c + 2.2, floor_exp, p)
            g = 2 * U * p + 17
            for j, slot in enumerate(Z_SLOTS):
                t = g + slot + .3
                at("tensor", t, z_step, p, j)
                at("scalar", t + .4, relu_step, p, j)
                at("vector", t + .65, h_full_step, p, j)
                at("scalar", t + 1.0, h_hi_step, p, j)
                at("gpsimd", t + 1.2, h_lo_step, p, j)
                at("tensor", t + 2.3, y_step, p, j)
            e = t + 2.7
            at("scalar", e, y_out, p)
            at("vector", e + .5, spikes_step, p)
            use_misc(e + 1.6, spikes_T, ("s", p), p)
            at("vector", e + 1.8, out_step, p)
            at("sync", e + 2.2, store, p)
            at("sync", e + 2.25, out_mark, p)

        block = ctx.enter_context(nc.Block())

        @block.sync
        def _(eng):
            play("sync", eng)
            landed(eng, "stored", 0, PAIRS - 1, 2)

        @block.scalar
        def _(eng):
            play("scalar", eng)

        @block.vector
        def _(eng):
            play("vector", eng)

        @block.tensor
        def _(eng):
            play("tensor", eng)

        @block.gpsimd
        def _(eng):
            play("gpsimd", eng)


def kernel(x, ctx_1024, g_xattn, g_ffn, L0_xattn_igate_w, L0_xattn_igate_b, L0_xattn_fgate_w, L0_xattn_fgate_b,
           L0_xattn_ln_scale, L0_ffn_W_fc, L0_ffn_W_proj):
    import concourse.bacc as bacc
    from concourse.bass_utils import run_bass_kernel_spmd

    arrays = {
        "x": x,
        "ctx_rows": ctx_1024,
        "ctx_cols": np.transpose(ctx_1024, (0, 2, 1)),
        "g_xattn": g_xattn,
        "g_ffn": g_ffn,
        "gate_w": np.transpose(np.concatenate([L0_xattn_igate_w, L0_xattn_fgate_w], axis=0)),
        "gate_b": np.stack([L0_xattn_igate_b, L0_xattn_fgate_b]),
        "ln_scale": L0_xattn_ln_scale,
        "w_fc_t": np.transpose(L0_ffn_W_fc),
        "w_proj_t": np.transpose(L0_ffn_W_proj),
    }
    arrays = {n: np.ascontiguousarray(a) for n, a in arrays.items()}
    nc = bacc.Bacc("TRN2", target_bir_lowering=False, num_devices=1)
    args = [nc.dram_tensor(n, a.shape, mybir.dt.from_np(a.dtype), kind="ExternalInput").ap() for n, a in arrays.items()]
    out = nc.dram_tensor("out", x.shape, mybir.dt.float32, kind="ExternalOutput").ap()
    build_block(nc, *args, out)
    r = run_bass_kernel_spmd(nc, [arrays], core_ids=[0])
    return r.results[0]["out"]
```

```python
from contextlib import ExitStack

import numpy as np
import concourse.bass as bass
from concourse import mybir


PLAN = {
    "arg": 0, "qk": 0.05, "decay": 0.45, "cmul": 0.7, "c_hi": 1.15, "c_lo": 1.75,
    "load": -18.8, "ln1_stats": -14.85, "ln1_rstd": -14.45, "xln": -13.6, "q_T": -12.75, "q_hi": -12.45, "q_lo": -12,
    "k_hi": -13.1, "k_lo": -13.15, "gates": -11.35, "gates_out": -11, "stack": -7.45, "load_v": -12.65, "v_hi": -6.25, "v_lo": -6.4,
    "gate_T": -4.95, "gate_softplus": -4.25, "gate_pre": -4.15, "gate_cumsum": -3.45, "gate_cummax": -3.05, "am_split0": -2.65, "am_split1": -2.45,
    "am_split2": -2.25, "am_split3": -2.05,
    "am_rows": -1.35, "floor_T": -2.55, "floor_exp": -2.15,
    "pv0": 5.35, "pv1": 7.75, "h_norm": 8.6, "ln2_stats": 10, "ln2_rstd": 10.75, "x1": 11.1, "ln3_stats": 12.45,
    "ln3_rstd": 12.95, "x1ln": 13.3, "x2_T": 14.5, "x2_hi": 14.7, "x2_lo": 15.4,
    "ffn": 21.95, "tile0": 0, "tile1": 1, "tile2": 3, "tile3": 4, "tile4": 6, "tile5": 7, "tile6": 9, "tile7": 10,
    "z": -0.1, "relu": 0.2, "h_full": 0.55, "h_hi": 0.95, "h_lo": 1.15, "y": 2.5,
    "y_out": 3.2, "spikes": 3.55, "spikes_every": 0.8, "spikes_T": 9.95, "out": 10.15, "store": 10.75,
}
ON = {"k_hi": "scalar", "k_lo": "gpsimd", "v_hi": "scalar", "v_lo": "gpsimd", "am_cast": "scalar", "am_rest": "vector"}
SQUARES_ON_ACT = (3, 7)


def lif_thresholds(beta, threshold, steps, top=4.0):
    one, b, th = np.float32(1), np.float32(beta), np.float32(threshold)

    def count(y):
        mem, n = np.float32(0), 0
        for _ in range(steps):
            reset = one if mem - th > 0 else np.float32(0)
            mem = np.float32(np.float32(np.float32(b * mem) + y) - reset * th)
            n += int(mem - th > 0)
        return n

    found = []
    for n in range(1, steps + 1):
        lo, hi = np.float32(0), np.float32(top)
        while True:
            mid = np.float32((float(lo) + float(hi)) / 2)
            if mid == lo or mid == hi:
                break
            lo, hi = (lo, mid) if count(mid) >= n else (mid, hi)
        found.append(float(lo))
    return found


def build_block(nc, x, ctx_rows, ctx_cols, g_xattn, g_ffn, gate_w, gate_b, ln_scale, w_fc_t, w_proj_t, out):
    fp32, bf16, fp32r = mybir.dt.float32, mybir.dt.bfloat16, mybir.dt.float32r
    ALU, ACT = mybir.AluOpType, mybir.ActivationFunctionType

    P = 128
    B, S, D = x.shape
    NH = gate_b.shape[1]
    DH = D // NH
    F = w_fc_t.shape[1]
    ST = S // P
    DC = D // P
    HPC = P // DH
    FT = F // P
    PAIRS = B // 2
    PT = 2 * S
    BANK = 512
    VW = DH + 1
    EPS, LN_EPS = 1e-6, 1e-5
    MASKED = -1.0e30
    LOG_QK_SCALE = -0.5 * float(np.log(DH))
    THETA = lif_thresholds(0.9, 1.0, 5)
    STEPS = len(THETA)

    UNITS = [(0, (0, 1)), (0, (2, 3)), (1, (0, 1, 2, 3)), (0, (4, 5)), (0, (6, 7)), (1, (4, 5, 6, 7))]
    U = len(UNITS)

    NX, NC, NQ, NST, NV, NAM, NUN, NCH, NX1, NX2, NHF, NRE = 5, 2, 2, 3, 3, 3, 3, 6, 3, 2, 2, 3

    with ExitStack() as ctx:
        def sb(name, shape, dt):
            return ctx.enter_context(nc.sbuf_tensor(name, shape, dt))

        def ps(name, shape, dt=fp32):
            return ctx.enter_context(nc.psum_tensor(name, shape, dt))

        ident = sb("ident", [P, P], fp32)
        ident_b = sb("ident_b", [P, P], bf16)
        behind = sb("behind", [P, P], bf16)
        scale_row = sb("scale_row", [P, D], fp32)
        g_col = sb("g_col", [P, 2], fp32)
        tanh_g = sb("tanh_g", [P, 2], fp32)
        rate_g = sb("rate_g", [P, 1], fp32)
        eps_col = sb("eps_col", [P, 1], fp32)
        lqk_col = sb("lqk_col", [P, 1], fp32)
        ibias = sb("ibias", [2 * NH, 1], fp32)
        fbias = sb("fbias", [2 * NH, 1], fp32)
        gw_raw = sb("gw_raw", [P, 3 * DC, 2 * NH], fp32)
        gw_sum = sb("gw_sum", [P, 2 * DC, 2 * NH], fp32)
        gw_hi = sb("gw_hi", [P, 2 * DC, 2 * NH], bf16)
        gw_lo = sb("gw_lo", [P, 2 * DC, 2 * NH], bf16)
        w_raw = sb("w_raw", [P, DC * F], fp32)
        wfc_hi = sb("wfc_hi", [P, DC, F], fp32r)
        wfc_lo = sb("wfc_lo", [P, DC, F], fp32r)
        wpr_hi = sb("wpr_hi", [P, FT, D], fp32r)
        wpr_lo = sb("wpr_lo", [P, FT, D], fp32r)

        x_in = [sb(f"x_in{i}", [P, ST, D], fp32) for i in range(NX)]
        v_in = [sb(f"v_in{i}", [P, ST, D], fp32) for i in range(NC)]
        kT_in = [sb(f"kT_in{i}", [P, DC, S], fp32) for i in range(NC)]
        stat1 = sb("stat1", [P, ST, 6], fp32)
        mv1 = [sb(f"mv1_{i}", [P, ST, 2], fp32) for i in range(2)]
        rstd1 = [sb(f"rstd1_{i}", [P, ST], fp32) for i in range(2)]
        lnv1 = sb("lnv1", [P, ST], fp32)
        xln = sb("xln", [P, ST, D], fp32)
        qT_hi = [sb(f"qT_hi{i}", [P, DC, S], bf16) for i in range(NQ)]
        qT_lo = [sb(f"qT_lo{i}", [P, DC, S], bf16) for i in range(NQ)]
        kT_hi = [sb(f"kT_hi{i}", [P, DC, S], bf16) for i in range(NQ)]
        kT_lo = [sb(f"kT_lo{i}", [P, DC, S], bf16) for i in range(NQ)]
        q_stack = [sb(f"q_stack{i}", [P, HPC, DC, S], bf16) for i in range(NST)]
        k_stack = [sb(f"k_stack{i}", [P, HPC, DC, S], bf16) for i in range(NST)]
        v_hi = [sb(f"v_hi{i}", [P, ST, NH, VW], bf16) for i in range(NV)]
        v_lo = [sb(f"v_lo{i}", [P, ST, NH, DH], bf16) for i in range(NV)]

        R = 2 * NH
        gates = [sb(f"gates{i}", [P, 2, ST, R], fp32) for i in range(2)]
        f_neg = sb("f_neg", [R, S], fp32)
        i_pre = sb("i_pre", [R, S], fp32)
        f_log = sb("f_log", [R, S], fp32)
        cs = sb("cs", [R, S], fp32)
        am = sb("am", [R, 2, S], fp32)
        row_max = sb("row_max", [R, S], fp32)
        am_rest = sb("am_rest", [R, 2, S], fp32)
        am_part = sb("am_part", [R, 3, 2, S], bf16)
        a_rows = [sb(f"a_rows{i}", [P, NH, S], bf16) for i in range(NAM)]
        m_rows = [sb(f"m_rows{i}", [P, NH, S], bf16) for i in range(NAM)]
        floor = [sb(f"floor{i}", [P, ST, R], fp32) for i in range(3)]

        decay = [sb(f"decay{i}", [P, BANK], fp32) for i in range(NUN)]
        c_hi = [sb(f"c_hi{i}", [P, BANK], bf16) for i in range(NCH)]
        c_lo = [sb(f"c_lo{i}", [P, BANK], bf16) for i in range(NCH)]

        denom = sb("denom", [P, ST, NH], fp32)
        rdenom = sb("rdenom", [P, ST, NH], fp32)
        h_rows = sb("h_rows", [P, ST, D], fp32)
        stat2 = sb("stat2", [P, ST, 6], fp32)
        mv2 = sb("mv2", [P, ST, 2], fp32)
        lnv2 = sb("lnv2", [P, ST], fp32)
        rstd2 = sb("rstd2", [P, ST], fp32)
        rstd2g = sb("rstd2g", [P, ST], fp32)
        x1 = [sb(f"x1_{i}", [P, 2 * ST, D], fp32) for i in range(NX1)]
        stat3 = sb("stat3", [P, ST, 6], fp32)
        mv3 = sb("mv3", [P, ST, 2], fp32)
        lnv3 = sb("lnv3", [P, ST], fp32)
        rstd3 = sb("rstd3", [P, ST], fp32)
        x1ln = sb("x1ln", [P, ST, D], fp32)
        x2_hi = [sb(f"x2_hi{i}", [P, DC, PT], fp32r) for i in range(NX2)]
        x2_lo = [sb(f"x2_lo{i}", [P, DC, PT], fp32r) for i in range(NX2)]

        relu = [sb(f"relu{i}", [P, PT], fp32) for i in range(NRE)]
        h_hi = [sb(f"h_hi{i}", [P, PT], fp32r) for i in range(NHF)]
        h_lo = [sb(f"h_lo{i}", [P, PT], fp32r) for i in range(NHF)]
        y_sb = w_raw[:, 0:DC * PT].rearrange("p (c s) -> p c s", c=DC)
        spikes = sb("spikes", [P, DC, PT], bf16)
        out_sb = w_raw[:, DC * PT:2 * DC * PT].rearrange("p (t d) -> p t d", d=D)

        arg_ps = ps("arg_ps", [P, BANK])
        qk_ps = ps("qk_ps", [P, BANK])
        z_ps = ps("z_ps", [P, BANK])
        misc_ps = ps("misc_ps", [P, BANK])
        pv_ps = ps("pv_ps", [P, ST, BANK])
        y_ps = ps("y_ps", [P, DC, BANK])
        misc_spikes = misc_ps[:, :].bitcast(bf16).rearrange("p (t d) -> p t d", d=D)
        pv_heads = pv_ps[:, :, 0:NH * VW].rearrange("p t (h c) -> p t h c", c=VW)

        sems = {}

        def sem(name):
            if name not in sems:
                sems[name] = ctx.enter_context(nc.semaphore(name))
            return sems[name]

        def after(eng, stage, n):
            if n >= 0:
                eng.wait_ge(sem(stage), n + 1)

        def landed(eng, ring, slot, n, dmas):
            eng.wait_ge(sem(f"{ring}{slot}"), 16 * dmas * (n + 1))

        streams = {k: [] for k in ("sync", "scalar", "vector", "tensor", "gpsimd")}

        def at(engine, time, step, *args):
            streams[engine].append((round(time, 3), len(streams[engine]), step, args))

        def play(engine, eng):
            for _, _, step, args in sorted(streams[engine], key=lambda e: e[:2]):
                step(eng, *args)

        chains = {}

        def link(eng, which, ins):
            chains[which] = chains.get(which, 0) + 1
            ins.then_inc(sem(f"chain_{which}"), 1)
            eng.wait_ge(sem(f"chain_{which}"), chains[which])

        misc_users = []

        def misc_turn(eng, user):
            after(eng, "misc_free", misc_use(user) - 1)

        def setup_loads(e):
            e.dma_start(w_raw[:, :], w_fc_t.rearrange("(c p) f -> p c f", p=P)).then_inc(sem("ld_wfc"), 16)
            e.dma_start(gw_raw[:, :, :], gate_w.rearrange("(c p) g -> p c g", p=P)).then_inc(sem("ld_small"), 16)
            e.dma_start(scale_row[:, :], ln_scale.partition_broadcast(P)).then_inc(sem("ld_small"), 16)
            e.dma_start(g_col[:, 0:1], g_xattn.partition_broadcast(P)).then_inc(sem("ld_small"), 16)
            e.dma_start(g_col[:, 1:2], g_ffn.partition_broadcast(P)).then_inc(sem("ld_small"), 16)
            for b in range(2):
                for row, col in enumerate((ibias, fbias)):
                    e.dma_start(col[b * NH:(b + 1) * NH, :], gate_b[row, :].unsqueeze(1)).then_inc(sem("ld_small"), 16)
        SMALL_LOADS = 8 * 16

        def setup_load_wproj(e):
            after(e, "wfc_ready", 0)
            e.dma_start(w_raw[:, :], w_proj_t.rearrange("(j p) d -> p j d", p=P)).then_inc(sem("ld_wpr"), 16)

        def setup_pool(e):
            e.memset(ident[:, :], 0.0).then_inc(sem("zeroed"), 1)
            e.memset(ident_b[:, :], 0.0).then_inc(sem("zeroed"), 1)
            e.memset(behind[:, :], 0.0).then_inc(sem("zeroed"), 1)
            for t in v_hi:
                last = e.memset(t[:, :, :, DH:VW], 1.0)
            last.then_inc(sem("zeroed"), 1)
            e.wait_ge(sem("zeroed"), 4)
            e.affine_select(out=behind[:, :], in_=behind[:, :], compare_op=ALU.is_ge, fill=MASKED, base=0,
                            pattern=[[1, P]], channel_multiplier=-1).then_inc(sem("ident_ready"), 1)
            for t in (ident, ident_b):
                e.affine_select(out=t[:, :], in_=t[:, :], compare_op=ALU.not_equal, fill=1.0, base=0,
                                pattern=[[-1, P]], channel_multiplier=1).then_inc(sem("ident_ready"), 1)

        def setup_rows(e):
            def pair_of(value):
                top = int(np.array([value], np.float32).view(np.uint32)[0]) >> 16
                return float(np.array([top << 16 | top], np.uint32).view(np.float32)[0])

            def flat(t):
                return t[:, :, :].rearrange("p h s -> p (h s)").bitcast(fp32)

            for t in m_rows:
                link(e, "gpsimd", e.memset(flat(t), 0.0))
                e.memset(flat(t)[0:3, :], pair_of(1.0))
            for t in a_rows:
                last = e.memset(flat(t), pair_of(-1.0))
            last.then_inc(sem("rows_ready"), 1)

        def setup_vector(e):
            e.memset(eps_col[:, :], LN_EPS)
            e.memset(lqk_col[:, :], LOG_QK_SCALE).then_inc(sem("cols_ready"), 1)
            e.wait_ge(sem("ld_small"), SMALL_LOADS)
            e.tensor_copy(gw_sum[:, 0:DC, :], gw_raw[:, 0:DC, :])
            link(e, "vector", e.tensor_tensor(gw_sum[:, DC:, :], gw_raw[:, DC:2 * DC, :], gw_raw[:, 2 * DC:, :], ALU.add))
            link(e, "vector", e.tensor_copy(gw_hi[:, :, :], gw_sum[:, :, :]))
            e.tensor_tensor(gw_lo[:, :, :], gw_sum[:, :, :], gw_hi[:, :, :], ALU.subtract).then_inc(sem("gw_ready"), 1)
            after(e, "tanh_ready", 0)
            e.tensor_scalar(rate_g[:, :], tanh_g[:, 1:2], 1.0 / STEPS, None, ALU.mult)

        def split_weights(e, stage, load, hi, lo):
            e.wait_ge(sem(load), 16)
            flat = "p a b -> p (a b)"
            link(e, "vector", e.tensor_copy(hi[:, :, :].rearrange(flat), w_raw[:, :]))
            e.tensor_tensor(lo[:, :, :].rearrange(flat), w_raw[:, :], hi[:, :, :].bitcast(fp32).rearrange(flat),
                            ALU.subtract).then_inc(sem(stage), 1)

        def setup_tanh(e):
            e.wait_ge(sem("ld_small"), SMALL_LOADS)
            e.activation(tanh_g[:, :], g_col[:, :], ACT.Tanh).then_inc(sem("tanh_ready"), 1)
            e.preload_act_table_set("natural_log_exp_and_others")

        def load_batch(e, b):
            after(e, "x1_done", b - NX)
            e.dma_start(x_in[b % NX][:, :, :], x[b].rearrange("(t p) d -> p t d", p=P)).then_inc(sem(f"ld_x{b % NX}"), 16)
            after(e, "k_split", b - NC)
            e.dma_start(kT_in[b % NC][:, :, :], ctx_cols[b]).then_inc(sem(f"ld_k{b % NC}"), 16)

        def load_values(e, b):
            after(e, "v_split", b - NC)
            e.dma_start(v_in[b % NC][:, :, :], ctx_rows[b].rearrange("(t p) d -> p t d", p=P)).then_inc(sem(f"ld_v{b % NC}"), 16)

        def row_stats(e, src, stat, mv):
            for t in range(ST):
                ins = e.bn_stats(stat[:, t, :], src[:, t, :])
            link(e, "vector", ins)
            for t in range(ST):
                ins = e.bn_aggr(mv[:, t, :], stat[:, t, :])
            return ins

        def rstd_of(e, rstd, lnv, mv):
            link(e, "scalar", e.activation(lnv[:, :], mv[:, :, 1], ACT.Ln, bias=eps_col[:, :]))
            return e.activation(rstd[:, :], lnv[:, :], ACT.Exp, scale=-0.5)

        def normalise(e, dst, src, mv, rstd):
            for t in range(ST):
                ins = e.tensor_scalar(dst[:, t, :], src[:, t, :], mv[:, t, 0:1], rstd[:, t:t + 1], ALU.subtract, ALU.mult)
            return ins

        def ln1_stats(e, b):
            landed(e, "ld_x", b % NX, b // NX, 1)
            after(e, "xln", b - 2)
            row_stats(e, x_in[b % NX], stat1, mv1[b % 2]).then_inc(sem("ln1_stats"), 1)

        def ln1_rstd(e, b):
            after(e, "cols_ready", 0)
            after(e, "ln1_stats", b)
            after(e, "xln", b - 2)
            rstd_of(e, rstd1[b % 2], lnv1, mv1[b % 2]).then_inc(sem("ln1_rstd"), 1)

        def ln1_apply(e, b):
            after(e, "ln1_rstd", b)
            after(e, "q_T", b - 1)
            for t in range(ST):
                ins = e.tensor_scalar(xln[:, t, :].rearrange("p (c d g) -> p c g d", c=DC, g=HPC),
                                      x_in[b % NX][:, t, :].rearrange("p (c g d) -> p c g d", c=DC, g=HPC),
                                      mv1[b % 2][:, t, 0:1], rstd1[b % 2][:, t:t + 1], ALU.subtract, ALU.mult)
            ins.then_inc(sem("xln"), 1)

        def cast(e, step, dst, src):
            if ON[step] == "scalar":
                return e.activation(dst, src, ACT.Copy)
            if ON[step] == "vector":
                return e.tensor_copy(dst, src)
            return e.tensor_scalar(dst, src, 1.0, 1.0, ALU.mult, ALU.mult)

        def k_hi(e, b):
            landed(e, "ld_k", b % NC, b // NC, 1)
            after(e, "gates", b - NQ)
            if b >= NQ:
                landed(e, "ld_stack", (b - NQ) % NST, (b - NQ) // NST, STACK_DMAS)
            cast(e, "k_hi", kT_hi[b % NQ][:, :, :], kT_in[b % NC][:, :, :]).then_inc(sem("k_hi"), 1)

        def k_lo(e, b):
            after(e, "k_hi", b)
            e.tensor_tensor(kT_lo[b % NQ][:, :, :], kT_in[b % NC][:, :, :], kT_hi[b % NQ][:, :, :],
                            ALU.subtract).then_inc(sem("k_split"), 1)

        def v_heads(b):
            return v_in[b % NC][:, :, :].rearrange("p t (h d) -> p t h d", d=DH), v_hi[b % NV][:, :, :, 0:DH]

        def v_hi_step(e, b):
            landed(e, "ld_v", b % NC, b // NC, 1)
            after(e, "pv", 2 * (b - NV) + 1)
            src, hi = v_heads(b)
            cast(e, "v_hi", hi, src).then_inc(sem("v_hi"), 1)

        def v_lo_step(e, b):
            after(e, "v_hi", b)
            src, hi = v_heads(b)
            e.tensor_tensor(v_lo[b % NV][:, :, :, :], src, hi, ALU.subtract).then_inc(sem("v_split"), 1)

        def transpose_rows(e, src):
            for c in range(DC):
                for t in range(ST):
                    col = c * S + t * P
                    ins = e.transpose(misc_ps[:, col:col + P], src[:, t, c * P:(c + 1) * P], ident[:, :])
            return ins

        def q_T(e, b):
            e.wait_ge(sem("ident_ready"), 3)
            after(e, "xln", b)
            misc_turn(e, ("q", b))
            transpose_rows(e, xln).then_inc(sem("q_T"), 1)

        def misc_chunks():
            return misc_ps[:, :].rearrange("p (c s) -> p c s", c=DC)

        def q_hi(e, b):
            after(e, "q_T", b)
            after(e, "gates", b - NQ)
            if b >= NQ:
                landed(e, "ld_stack", (b - NQ) % NST, (b - NQ) // NST, STACK_DMAS)
            e.activation(qT_hi[b % NQ][:, :, :], misc_chunks(), ACT.Copy).then_inc(sem("q_hi"), 1)

        def q_lo(e, b):
            after(e, "q_hi", b)
            e.tensor_tensor(qT_lo[b % NQ][:, :, :], misc_chunks(), qT_hi[b % NQ][:, :, :],
                            ALU.subtract).then_inc(sem("misc_free"), 1)

        def misc_use(user):
            return [u for _, _, u in sorted(misc_users)].index(user)

        STACK_Q = ((0, qT_hi), (2, qT_hi), (1, qT_lo), (3, qT_lo))
        STACK_K = ((0, kT_hi), (1, kT_hi), (2, kT_lo), (3, kT_lo))
        STACK_DMAS = len(STACK_Q) + len(STACK_K)

        def stack_heads(e, b):
            slot = b % NST
            done = sem(f"ld_stack{slot}")
            after(e, "k_split", b)
            after(e, "misc_free", misc_use(("q", b)))
            after(e, "cmul", U * (b - NST) + U - 1)
            for stack, parts in ((k_stack, STACK_K), (q_stack, STACK_Q)):
                for j, part in parts:
                    dst = stack[slot][DH * j:DH * (j + 1), :, :, :].rearrange("d g c s -> d g (c s)")
                    e.dma_start(dst, part[b % NQ][:, :, :].rearrange("p c s -> p (c s)")).then_inc(done, 16)

        def gate_products(e, b):
            after(e, "gw_ready", 0)
            after(e, "k_split", b)
            after(e, "misc_free", misc_use(("q", b)))
            misc_turn(e, ("g", b))
            n = b % NQ
            for t in range(ST):
                terms = [(part[n][:, c, t * P:(t + 1) * P], w[:, k * DC + c, :])
                         for k, (hi, lo) in enumerate(((qT_hi, qT_lo), (kT_hi, kT_lo)))
                         for c in range(DC)
                         for part, w in ((hi, gw_hi), (hi, gw_lo), (lo, gw_hi))]
                for i, (lhsT, rhs) in enumerate(terms):
                    ins = e.matmul(misc_ps[:, t * R:(t + 1) * R], lhsT, rhs, start=(i == 0), stop=(i == len(terms) - 1))
            ins.then_inc(sem("gates"), 1)

        def gates_out(e, b):
            after(e, "gates", b)
            after(e, "gate_T", b // 2 - 2)
            src = misc_ps[:, 0:ST * R].rearrange("p (t k h) -> p k t h", t=ST, k=2)
            e.activation(gates[b // 2 % 2][:, :, :, b % 2 * NH:(b % 2 + 1) * NH], src, ACT.Copy).then_inc(sem("misc_free"), 1)

        def gate_T(e, p):
            after(e, "misc_free", misc_use(("g", 2 * p + 1)))
            misc_turn(e, ("gT", p))
            for k in range(2):
                for t in range(ST):
                    col = k * S + t * P
                    ins = e.transpose(misc_ps[0:R, col:col + P], gates[p % 2][:, k, t, :], ident[:, :])
            ins.then_inc(sem("gate_T"), 1)

        def gate_softplus(e, p):
            after(e, "gate_T", p)
            after(e, "gate_cummax", p - 1)
            ins = e.activation(f_log[:, :], misc_ps[0:R, S:2 * S], ACT.Abs, bias=fbias[:, :])
            ins.then_inc(sem("gate_abs"), 1)
            after(e, "gate_abs", p)
            link(e, "scalar", e.activation(f_log[:, :], f_log[:, :], ACT.Exp, scale=-1.0))
            e.activation(f_log[:, :], f_log[:, :], ACT.Ln, bias=1.0).then_inc(sem("gate_softplus"), 1)

        def gate_pre(e, p):
            after(e, "gate_abs", p)
            e.tensor_scalar(f_neg[:, :], misc_ps[0:R, S:2 * S], fbias[:, :], 0.0, ALU.add, ALU.min)
            e.tensor_scalar(i_pre[:, :], misc_ps[0:R, 0:S], ibias[:, :], None, ALU.add).then_inc(sem("misc_free"), 1)

        def gate_cumsum(e, p):
            after(e, "gate_softplus", p)
            after(e, "misc_free", misc_use(("gT", p)))
            after(e, "am_split", 4 * p - 1)
            link(e, "vector", e.tensor_tensor_scan(cs[:, :], f_neg[:, :], f_log[:, :], 0.0, ALU.add, ALU.subtract))
            e.tensor_tensor(am[:, 0, :], i_pre[:, :], cs[:, :], ALU.subtract).then_inc(sem("gate_cumsum"), 1)

        def gate_cummax(e, p):
            after(e, "gate_cumsum", p)
            after(e, "floor_T", p - 1)
            a, m = am[:, 0, :], am[:, 1, :]
            link(e, "vector", e.tensor_tensor_scan(m, a, a, -3.0e38, ALU.max, ALU.max))
            e.tensor_tensor(row_max[:, :], m, cs[:, :], ALU.add).then_inc(sem("gate_cummax"), 1)

        def am_split(e, p, n):
            if n == 0:
                after(e, "gate_cummax", p)
                for b in (2 * p - 2, 2 * p - 1):
                    if b >= 0:
                        landed(e, "ld_am", b % NAM, b // NAM, AM_DMAS)
            else:
                after(e, "am_split", 4 * p + n - 1)
            src = am if n < 2 else am_rest
            hi = am_part[:, n // 2, :, :]
            if n % 2 == 0:
                ins = cast(e, "am_cast", hi, src[:, :, :])
            else:
                ins = e.tensor_tensor(am_rest[:, :, :] if n == 1 else am_part[:, 2, :, :], src[:, :, :], hi, ALU.subtract)
            ins.then_inc(sem("am_split"), 1)

        AM_DMAS = 6

        def am_rows(e, b):
            after(e, "rows_ready", 0)
            after(e, "am_split", 4 * (b // 2) + 3)
            after(e, "arg", U * (b - NAM + 1) - 1)
            mine = slice(b % 2 * NH, (b % 2 + 1) * NH)
            for k, (rows, first) in enumerate(((a_rows, 0), (m_rows, 3))):
                for j in range(3):
                    e.dma_start(rows[b % NAM][first + j:first + j + 1, :, :], am_part[mine, j, k, :])\
                     .then_inc(sem(f"ld_am{b % NAM}"), 16)

        def floor_T(e, p):
            after(e, "gate_cummax", p)
            misc_turn(e, ("fT", p))
            for t in range(ST):
                ins = e.transpose(misc_ps[:, t * R:(t + 1) * R], row_max[:, t * P:(t + 1) * P], ident[0:R, 0:R])
            ins.then_inc(sem("floor_T"), 1)

        def floor_exp(e, p):
            after(e, "floor_T", p)
            after(e, "h_norm", 2 * (p - 3) + 1)
            e.activation(floor[p % 3][:, :, :], misc_ps[:, 0:ST * R].rearrange("p (t r) -> p t r", t=ST), ACT.Exp,
                         scale=-1.0).then_inc(sem("misc_free"), 1)

        def unit_spans(kt, heads):
            n = S - kt * P
            return [(h, slice(i * n, (i + 1) * n), kt * P) for i, h in enumerate(heads)]

        def arg(e, b, u):
            kt, heads = UNITS[u]
            landed(e, "ld_am", b % NAM, b // NAM, AM_DMAS)
            after(e, "decay", b * U + u - 1)
            for h, cols, s0 in unit_spans(kt, heads):
                e.matmul(arg_ps[:, cols], a_rows[b % NAM][:, h, kt * P:(kt + 1) * P], m_rows[b % NAM][:, h, s0:S],
                         start=True, stop=False)
                ins = e.matmul(arg_ps[:, cols.start:cols.start + P], ident_b[:, :], behind[:, :], start=False, stop=True)
            ins.then_inc(sem("arg"), 1)

        def qk(e, b, u):
            kt, heads = UNITS[u]
            slot = b % NST
            landed(e, "ld_stack", slot, b // NST, STACK_DMAS)
            after(e, "cmul", b * U + u - 1)
            for h, cols, s0 in unit_spans(kt, heads):
                c, g = h // HPC, h % HPC
                ins = e.matmul(qk_ps[:, cols], k_stack[slot][:, g, c, kt * P:(kt + 1) * P], q_stack[slot][:, g, c, s0:S],
                               start=True, stop=True)
            ins.then_inc(sem("qk"), 1)

        def decay_exp(e, b, u):
            i = b * U + u
            after(e, "arg", i)
            after(e, "c_lo", i - NUN)
            e.activation(decay[i % NUN][:, :], arg_ps[:, :], ACT.Exp, bias=lqk_col[:, :]).then_inc(sem("decay"), 1)

        def cmul(e, b, u):
            i = b * U + u
            after(e, "qk", i)
            after(e, "decay", i)
            e.tensor_tensor(decay[i % NUN][:, :], qk_ps[:, :], decay[i % NUN][:, :], ALU.mult).then_inc(sem("cmul"), 1)

        def c_hi_step(e, b, u):
            i = b * U + u
            after(e, "cmul", i)
            after(e, "pv", (i - NCH) // 3)
            e.activation(c_hi[i % NCH][:, :], decay[i % NUN][:, :], ACT.Copy).then_inc(sem("c_hi"), 1)

        def c_lo_step(e, b, u):
            i = b * U + u
            after(e, "c_hi", i)
            e.tensor_tensor(c_lo[i % NCH][:, :], decay[i % NUN][:, :], c_hi[i % NCH][:, :], ALU.subtract).then_inc(sem("c_lo"), 1)

        def pv(e, b, half):
            first = half * 3
            after(e, "c_lo", b * U + first + 2)
            after(e, "v_split", b)
            if half == 0:
                after(e, "h_norm", b - 1)
            for qt in range(ST):
                for h in range(half * NH // 2, (half + 1) * NH // 2):
                    blocks = []
                    for u in range(first, first + 3):
                        kt, heads = UNITS[u]
                        if h in heads and kt <= qt:
                            col = heads.index(h) * (S - kt * P) + (qt - kt) * P
                            blocks.append((kt, (b * U + u) % NCH, col))
                    out_cols = pv_ps[:, qt, h * VW:(h + 1) * VW]
                    for n, (kt, slot, col) in enumerate(blocks):
                        hi, lo = c_hi[slot][:, col:col + P], c_lo[slot][:, col:col + P]
                        vh, vl = v_hi[b % NV][:, kt, h, :], v_lo[b % NV][:, kt, h, :]
                        e.matmul(out_cols, hi, vh, start=(n == 0), stop=False, skip_group_check=True)
                        e.matmul(pv_ps[:, qt, h * VW:h * VW + DH], hi, vl, start=False, stop=False, skip_group_check=True)
                        ins = e.matmul(out_cols, lo, vh, start=False, stop=(n == len(blocks) - 1), skip_group_check=True)
            ins.then_inc(sem("pv"), 1)

        def h_norm(e, b):
            p = b // 2
            after(e, "pv", 2 * b + 1)
            after(e, "misc_free", misc_use(("fT", p)))
            row_sum, least = pv_heads[:, :, :, DH], floor[p % 3][:, :, b % 2 * NH:(b % 2 + 1) * NH]
            link(e, "vector", e.scalar_tensor_tensor(denom[:, :, :], row_sum, -1.0, least, ALU.mult, ALU.max))
            link(e, "vector", e.tensor_tensor(denom[:, :, :], denom[:, :, :], row_sum, ALU.max))
            link(e, "vector", e.tensor_scalar(denom[:, :, :], denom[:, :, :], EPS, None, ALU.add))
            link(e, "vector", e.reciprocal(rdenom[:, :, :], denom[:, :, :]))
            heads = h_rows[:, :, :].rearrange("p t (h d) -> p t h d", d=DH)
            ins = e.tensor_tensor(heads, pv_heads[:, :, :, 0:DH],
                                  rdenom[:, :, :].unsqueeze(3).broadcast_to([P, ST, NH, DH]), ALU.mult)
            ins.then_inc(sem("h_norm"), 1)

        def ln2_stats(e, b):
            after(e, "h_norm", b)
            row_stats(e, h_rows, stat2, mv2).then_inc(sem("ln2_stats"), 1)

        def ln2_rstd(e, b):
            after(e, "ln2_stats", b)
            after(e, "x1_done", b - 1)
            rstd_of(e, rstd2, lnv2, mv2).then_inc(sem("ln2_rstd"), 1)

        def x1_step(e, b):
            after(e, "tanh_ready", 0)
            after(e, "ln2_rstd", b)
            after(e, "out_step", b // 2 - NX1)
            for t in range(ST):
                e.scalar_tensor_tensor(h_rows[:, t, :], h_rows[:, t, :], mv2[:, t, 0:1], scale_row[:, :],
                                       ALU.subtract, ALU.mult)
            link(e, "vector", e.tensor_scalar(rstd2g[:, :], rstd2[:, :], tanh_g[:, 0:1], None, ALU.mult))
            dst = x1[b // 2 % NX1][:, b % 2 * ST:(b % 2 + 1) * ST, :]
            for t in range(ST):
                ins = e.scalar_tensor_tensor(dst[:, t, :], h_rows[:, t, :], rstd2g[:, t:t + 1], x_in[b % NX][:, t, :],
                                             ALU.mult, ALU.add)
            ins.then_inc(sem("x1_done"), 1)

        def ln3_stats(e, b):
            after(e, "x1_done", b)
            after(e, "x1ln", b - 1)
            row_stats(e, x1[b // 2 % NX1][:, b % 2 * ST:(b % 2 + 1) * ST, :], stat3, mv3).then_inc(sem("ln3_stats"), 1)

        def ln3_rstd(e, b):
            after(e, "ln3_stats", b)
            after(e, "x1ln", b - 1)
            rstd_of(e, rstd3, lnv3, mv3).then_inc(sem("ln3_rstd"), 1)

        def ln3_apply(e, b):
            after(e, "ln3_rstd", b)
            after(e, "x2_T", b - 1)
            normalise(e, x1ln, x1[b // 2 % NX1][:, b % 2 * ST:(b % 2 + 1) * ST, :], mv3, rstd3).then_inc(sem("x1ln"), 1)

        def x2_T(e, b):
            after(e, "x1ln", b)
            misc_turn(e, ("x2", b))
            transpose_rows(e, x1ln).then_inc(sem("x2_T"), 1)

        def x2_cols(tiles, b):
            return tiles[b // 2 % NX2][:, :, b % 2 * S:(b % 2 + 1) * S]

        def x2_hi_step(e, b):
            after(e, "x2_T", b)
            after(e, "z", FT * (b // 2 - NX2 + 1) - 1)
            e.activation(x2_cols(x2_hi, b), misc_chunks(), ACT.Copy).then_inc(sem("x2_hi"), 1)

        def x2_lo_step(e, b):
            after(e, "x2_hi", b)
            e.tensor_tensor(x2_cols(x2_lo, b), misc_chunks(), x2_cols(x2_hi, b).bitcast(fp32),
                            ALU.subtract).then_inc(sem("misc_free"), 1)

        def z_step(e, p, j):
            if j == 0:
                after(e, "wfc_ready", 0)
                after(e, "misc_free", misc_use(("x2", 2 * p + 1)))
            after(e, "h_full", FT * p + j - 1)
            xh, xl = x2_hi[p % NX2], x2_lo[p % NX2]
            terms = [(w[:, c, j * P:(j + 1) * P], xx[:, c, :]) for c in range(DC)
                     for w, xx in ((wfc_hi, xh), (wfc_hi, xl), (wfc_lo, xh))]
            for n, (lhsT, rhs) in enumerate(terms):
                ins = e.matmul(z_ps[:, :], lhsT, rhs, start=(n == 0), stop=(n == len(terms) - 1))
            ins.then_inc(sem("z"), 1)

        def relu_step(e, p, j):
            n = FT * p + j
            after(e, "z", n)
            after(e, "h_lo", n - NRE)
            e.activation(relu[n % NRE][:, :], z_ps[:, :], ACT.Relu).then_inc(sem("relu"), 1)

        def h_full_step(e, p, j):
            n = FT * p + j
            after(e, "relu", n)
            r = relu[n % NRE][:, :]
            if j in SQUARES_ON_ACT:
                ins = e.activation(r, r, ACT.Square)
            else:
                ins = e.tensor_tensor(r, z_ps[:, :], r, ALU.mult)
            ins.then_inc(sem("h_full"), 1)

        def h_hi_step(e, p, j):
            n = FT * p + j
            after(e, "h_full", n)
            after(e, "y", n - NHF)
            e.activation(h_hi[n % NHF][:, :], relu[n % NRE][:, :], ACT.Copy).then_inc(sem("h_hi"), 1)

        def h_lo_step(e, p, j):
            n = FT * p + j
            after(e, "h_hi", n)
            e.tensor_tensor(h_lo[n % NHF][:, :], relu[n % NRE][:, :], h_hi[n % NHF][:, :].bitcast(fp32),
                            ALU.subtract).then_inc(sem("h_lo"), 1)

        def y_step(e, p, j):
            n = FT * p + j
            if j == 0:
                after(e, "wpr_ready", 0)
                after(e, "y_out", p - 1)
            after(e, "h_lo", n)
            hh, hl = h_hi[n % NHF], h_lo[n % NHF]
            for c in range(DC):
                terms = [(w[:, j, c * P:(c + 1) * P], h[:, :]) for w, h in ((wpr_hi, hh), (wpr_hi, hl), (wpr_lo, hh))]
                for i, (lhsT, rhs) in enumerate(terms):
                    ins = e.matmul(y_ps[:, c, :], lhsT, rhs, start=(j == 0 and i == 0),
                                   stop=(j == FT - 1 and i == len(terms) - 1))
            ins.then_inc(sem("y"), 1)

        def y_out(e, p):
            after(e, "y", FT * p + FT - 1)
            after(e, "spikes", STEPS * p - 1)
            e.activation(y_sb[:, :, :], y_ps[:, :, :], ACT.Copy).then_inc(sem("y_out"), 1)

        def spikes_step(e, p, n):
            if n == 0:
                after(e, "y_out", p)
                after(e, "spikes_T", p - 1)
                ins = e.tensor_scalar(spikes[:, :, :], y_sb[:, :, :], THETA[0], None, ALU.is_gt)
            else:
                after(e, "spikes", STEPS * p + n - 1)
                ins = e.scalar_tensor_tensor(spikes[:, :, :], y_sb[:, :, :], THETA[n], spikes[:, :, :], ALU.is_gt, ALU.add)
            ins.then_inc(sem("spikes"), 1)

        def spikes_T(e, p):
            after(e, "spikes", STEPS * (p + 1) - 1)
            misc_turn(e, ("s", p))
            for t in range(2 * ST):
                for c in range(DC):
                    ins = e.transpose(misc_spikes[:, t, c * P:(c + 1) * P], spikes[:, c, t * P:(t + 1) * P], ident_b[:, :])
            ins.then_inc(sem("spikes_T"), 1)

        def out_step(e, p):
            after(e, "spikes_T", p)
            if p >= 1:
                landed(e, "stored", 0, p - 1, 2)
            e.scalar_tensor_tensor(out_sb[:, :, :], misc_spikes, rate_g[:, :], x1[p % NX1][:, :, :], ALU.mult, ALU.add)\
             .then_inc(sem("misc_free"), 1)

        def out_mark(e, p):
            after(e, "misc_free", misc_use(("s", p)))
            e.sem_inc(sem("out_step"), 1)

        def store(e, p):
            after(e, "misc_free", misc_use(("s", p)))
            for b in range(2):
                e.dma_start(out[2 * p + b].rearrange("(t p) d -> p t d", p=P), out_sb[:, b * ST:(b + 1) * ST, :])\
                 .then_inc(sem("stored0"), 16)

        at("sync", -1e3, setup_loads)
        at("sync", -12.5, setup_load_wproj)
        at("gpsimd", -1e3, setup_pool)
        at("gpsimd", -13.5, setup_rows)
        at("vector", -1e3, setup_vector)
        at("scalar", -1e3, setup_tanh)
        at("vector", -10.9, split_weights, "wfc_ready", "ld_wfc", wfc_hi, wfc_lo)
        at("vector", -2, split_weights, "wpr_ready", "ld_wpr", wpr_hi, wpr_lo)

        def use_misc(time, step, user, *args):
            misc_users.append((round(time, 3), len(streams["tensor"]), user))
            at("tensor", time, step, *args)

        for b in range(B):
            t0 = U * b
            t = {name: t0 + offset for name, offset in PLAN.items()}
            at("sync", t["load"], load_batch, b)
            at("vector", t["ln1_stats"], ln1_stats, b)
            at("scalar", t["ln1_rstd"], ln1_rstd, b)
            at("vector", t["xln"], ln1_apply, b)
            at(ON["k_hi"], t["k_hi"], k_hi, b)
            at(ON["k_lo"], t["k_lo"], k_lo, b)
            at("sync", t["load_v"], load_values, b)
            at(ON["v_hi"], t["v_hi"], v_hi_step, b)
            at(ON["v_lo"], t["v_lo"], v_lo_step, b)
            use_misc(t["q_T"], q_T, ("q", b), b)
            at("scalar", t["q_hi"], q_hi, b)
            at("vector", t["q_lo"], q_lo, b)
            at("sync", t["stack"], stack_heads, b)
            use_misc(t["gates"], gate_products, ("g", b), b)
            at("scalar", t["gates_out"], gates_out, b)
            at("sync", t["am_rows"], am_rows, b)
            for u in range(U):
                at("tensor", t["arg"] + u, arg, b, u)
                at("tensor", t["qk"] + u, qk, b, u)
                at("scalar", t["decay"] + u, decay_exp, b, u)
                at("vector", t["cmul"] + u, cmul, b, u)
                at("scalar", t["c_hi"] + u, c_hi_step, b, u)
                at("gpsimd", t["c_lo"] + u, c_lo_step, b, u)
            at("tensor", t["pv0"], pv, b, 0)
            at("tensor", t["pv1"], pv, b, 1)
            at("vector", t["h_norm"], h_norm, b)
            at("vector", t["ln2_stats"], ln2_stats, b)
            at("scalar", t["ln2_rstd"], ln2_rstd, b)
            at("vector", t["x1"], x1_step, b)
            at("vector", t["ln3_stats"], ln3_stats, b)
            at("scalar", t["ln3_rstd"], ln3_rstd, b)
            at("vector", t["x1ln"], ln3_apply, b)
            use_misc(t["x2_T"], x2_T, ("x2", b), b)
            at("scalar", t["x2_hi"], x2_hi_step, b)
            at("vector", t["x2_lo"], x2_lo_step, b)
        for p in range(PAIRS):
            t0 = 2 * U * p
            t = {name: t0 + offset for name, offset in PLAN.items()}
            use_misc(t["gate_T"], gate_T, ("gT", p), p)
            at("scalar", t["gate_softplus"], gate_softplus, p)
            at("vector", t["gate_pre"], gate_pre, p)
            at("vector", t["gate_cumsum"], gate_cumsum, p)
            at("vector", t["gate_cummax"], gate_cummax, p)
            for n in range(4):
                at(ON["am_rest" if n % 2 else "am_cast"], t[f"am_split{n}"], am_split, p, n)
            use_misc(t["floor_T"], floor_T, ("fT", p), p)
            at("scalar", t["floor_exp"], floor_exp, p)
            for j in range(FT):
                z0 = t["ffn"] + PLAN[f"tile{j}"]
                at("tensor", z0 + PLAN["z"], z_step, p, j)
                at("scalar", z0 + PLAN["relu"], relu_step, p, j)
                at("scalar" if j in SQUARES_ON_ACT else "vector", z0 + PLAN["h_full"], h_full_step, p, j)
                at("scalar", z0 + PLAN["h_hi"], h_hi_step, p, j)
                at("gpsimd", z0 + PLAN["h_lo"], h_lo_step, p, j)
                at("tensor", z0 + PLAN["y"], y_step, p, j)
            at("scalar", z0 + PLAN["y_out"], y_out, p)
            for n in range(STEPS):
                at("vector", z0 + PLAN["spikes"] + n * PLAN["spikes_every"], spikes_step, p, n)
            use_misc(z0 + PLAN["spikes_T"], spikes_T, ("s", p), p)
            at("vector", z0 + PLAN["out"], out_step, p)
            at("sync", z0 + PLAN["store"], store, p)
            at("sync", z0 + PLAN["store"], out_mark, p)

        block = ctx.enter_context(nc.Block())

        @block.sync
        def _(eng):
            play("sync", eng)
            landed(eng, "stored", 0, PAIRS - 1, 2)

        @block.scalar
        def _(eng):
            play("scalar", eng)

        @block.vector
        def _(eng):
            play("vector", eng)

        @block.tensor
        def _(eng):
            play("tensor", eng)

        @block.gpsimd
        def _(eng):
            play("gpsimd", eng)


def kernel(x, ctx_1024, g_xattn, g_ffn, L0_xattn_igate_w, L0_xattn_igate_b, L0_xattn_fgate_w, L0_xattn_fgate_b,
           L0_xattn_ln_scale, L0_ffn_W_fc, L0_ffn_W_proj):
    import concourse.bacc as bacc
    from concourse.bass_utils import run_bass_kernel_spmd

    nh, d = L0_xattn_igate_w.shape[0], x.shape[2]
    dh, p = d // nh, 128

    def head_minor(a):
        return a.reshape(-1, p // dh, dh, a.shape[-1]).transpose(0, 2, 1, 3).reshape(a.shape)

    ctx_t = np.transpose(ctx_1024, (0, 2, 1))
    cols = head_minor(ctx_t.reshape(-1, ctx_t.shape[-1])).reshape(ctx_t.shape[0], d // p, p, -1)
    arrays = {
        "x": x,
        "ctx_rows": ctx_1024,
        "ctx_cols": np.transpose(cols, (0, 2, 1, 3)),
        "g_xattn": g_xattn,
        "g_ffn": g_ffn,
        "gate_w": head_minor(np.transpose(np.concatenate([L0_xattn_igate_w, L0_xattn_fgate_w], axis=0))),
        "gate_b": np.stack([L0_xattn_igate_b, L0_xattn_fgate_b]),
        "ln_scale": L0_xattn_ln_scale,
        "w_fc_t": np.transpose(L0_ffn_W_fc),
        "w_proj_t": np.transpose(L0_ffn_W_proj),
    }
    arrays = {n: np.ascontiguousarray(a) for n, a in arrays.items()}
    nc = bacc.Bacc("TRN2", target_bir_lowering=False, num_devices=1)
    args = [nc.dram_tensor(n, a.shape, mybir.dt.from_np(a.dtype), kind="ExternalInput").ap() for n, a in arrays.items()]
    out = nc.dram_tensor("out", x.shape, mybir.dt.float32, kind="ExternalOutput").ap()
    build_block(nc, *args, out)
    r = run_bass_kernel_spmd(nc, [arrays], core_ids=[0])
    return r.results[0]["out"]
```

```python
from contextlib import ExitStack

import numpy as np
import concourse.bass as bass
from concourse import mybir


PLAN = {
    "load_wfc": -4.03, "load_wproj": -2.25, "setup_gates": -11.06, "split_wfc": -4.27, "split_wproj": 3.76,
    "rows0": -15.6, "rows1": -4.67, "rows2": 0.18,
    "half0": 0.25, "half1": 12.45,
    "arg": (0, -0.46, -0.21, -0.04, 0.15, -0.07, -0.5, -0.24, 0.04, -0.24, -0.45, -0.77),
    "qk": (-0.13, 0.31, 0.04, 0.03, 0.17, -0.01, -0.36, 0.43, 0.5, 0.19, -0.23, -1.08),
    "decay": (0.54, 0.07, 0, 0.61, -0.27, -0.42, -0.95, -0.99, 0.1, -0.78, -0.27, 0.38),
    "cmul": (1.78, 1, 0.22, 0.72, 0.66, -0.16, -0.22, -0.18, 0.36, -0.02, -0.61, 0.97),
    "c_hi": (1.83, 1.57, 1.67, 1.41, 0.99, 0.14, 1.11, 0.2, 0.61, 0.8, 0.43, 0.87),
    "c_lo": (2.03, 1.51, 2.67, 1.97, 2.55, 1.69, 2.27, 1.39, 4.05, 3.63, 3.33, 2.37),
    "load": (-19.5, -20.55), "ln1_stats": (-14.04, -16.46), "ln1_rstd": (-12.76, -16.03), "xln": (-12.35, -14.87),
    "q_T": (-12.71, -13.64), "q_hi": (-11.01, -13.37), "q_lo": (-10.06, -12.87), "k_hi": (-16.39, -13.36),
    "k_lo": (-12.18, -12.29), "gates": (-10.04, -11.79), "gates_out": (-9.74, -12.82), "stack": (-10.24, -9.97),
    "load_v": (-9.8, -8.06), "v_hi": (1.9, 1.45), "v_lo": (2.03, 6.61), "am_rows": (-3.32, -7.64),
    "gate_T": -4.87, "gate_softplus": -5.71, "gate_pre": -5.16, "gate_cumsum": -4.67, "gate_cummax": -4.32,
    "am_split0": -3.85, "am_split1": -0.69, "am_split2": -2.56, "am_split3": -0.24, "floor_T": -1.67,
    "floor_exp": -1.02,
    "pv0": (5.33, 5.2), "pv1": (7.97, 6.83), "h_norm": (8.86, 8.19), "ln2_stats": (9.13, 9.87),
    "ln2_rstd": (10.12, 10.05), "x1": (10.4, 10.77), "ln3_stats": (12.04, 11.15), "ln3_rstd": (12.49, 11.22),
    "x1ln": (12.93, 12.52), "x2_T": (15.68, 14.28), "x2_hi": (15.72, 14.04), "x2_lo": (16.16, 14.31),
    "z": (21.16, 21.84, 22.78, 23.95, 25.47, 27.78, 30.39, 32.32),
    "relu": (21.71, 22.41, 23.54, 24.97, 26.65, 28.6, 30, 32.15),
    "h_full": (21.87, 23.85, 24.55, 25.58, 28.38, 29.72, 30.52, 32.71),
    "h_hi": (23.2, 24.95, 25.25, 26.74, 28.9, 29.56, 31.83, 33.24),
    "h_lo": (24.96, 25.96, 26.13, 27.85, 30.42, 31.64, 32.59, 35.33),
    "y": (24.47, 26.54, 28.19, 29.06, 31.9, 32.51, 33.75, 34.48),
    "y_out": 35.47, "spikes": (36.47, 36.77, 37.85, 38.27, 42.79), "out": 43.98, "store": 55.49,
}
ON = {
    "xln": "vector", "k_hi": "gpsimd", "k_lo": "gpsimd", "q_hi": "scalar", "gates_out": "scalar", "v_hi": "gpsimd",
    "v_lo": "gpsimd", "am_cast": "scalar", "am_rest": "gpsimd", "x1ln": "vector", "x2_hi": "scalar", "y_out": "scalar",
}
SQUARES_ON_ACT = (0, 1, 2, 3, 4, 6)


def lif_thresholds(beta, threshold, steps, top=4.0):
    one, b, th = np.float32(1), np.float32(beta), np.float32(threshold)

    def count(y):
        mem, n = np.float32(0), 0
        for _ in range(steps):
            reset = one if mem - th > 0 else np.float32(0)
            mem = np.float32(np.float32(np.float32(b * mem) + y) - reset * th)
            n += int(mem - th > 0)
        return n

    found = []
    for n in range(1, steps + 1):
        lo, hi = np.float32(0), np.float32(top)
        while True:
            mid = np.float32((float(lo) + float(hi)) / 2)
            if mid == lo or mid == hi:
                break
            lo, hi = (lo, mid) if count(mid) >= n else (mid, hi)
        found.append(float(lo))
    return found


def build_block(nc, x, ctx_rows, ctx_cols, g_both, gate_w, gate_b, ln_scale, w_fc_t, w_proj_t, out):
    fp32, bf16, fp32r = mybir.dt.float32, mybir.dt.bfloat16, mybir.dt.float32r
    ALU, ACT = mybir.AluOpType, mybir.ActivationFunctionType

    P = 128
    B, S, D = x.shape
    NH = gate_b.shape[0] // 2
    DH = D // NH
    F = w_fc_t.shape[1]
    ST = S // P
    DC = D // P
    HPC = P // DH
    FT = F // P
    PAIRS = B // 2
    PT = 2 * S
    BANK = 512
    VW = DH + 1
    EPS, LN_EPS = 1e-6, 1e-5
    MASKED = -1.0e30
    LOG_QK_SCALE = -0.5 * float(np.log(DH))
    THETA = lif_thresholds(0.9, 1.0, 5)
    STEPS = len(THETA)

    UNITS = [(0, (0, 1)), (0, (2, 3)), (1, (0, 1, 2, 3)), (0, (4, 5)), (0, (6, 7)), (1, (4, 5, 6, 7))]
    U = len(UNITS)

    NX, NC, NQ, NST, NV, NAM, NUN, NCH, NX1, NX2, NHF, NRE = 5, 2, 2, 3, 3, 3, 3, 6, 3, 2, 2, 3

    with ExitStack() as ctx:
        def sb(name, shape, dt):
            return ctx.enter_context(nc.sbuf_tensor(name, shape, dt))

        def ps(name, shape, dt=fp32):
            return ctx.enter_context(nc.psum_tensor(name, shape, dt))

        ident = sb("ident", [P, P], fp32)
        ident_b = sb("ident_b", [P, P], bf16)
        behind = sb("behind", [P, P], bf16)
        scale_row = sb("scale_row", [P, D], fp32)
        g_col = sb("g_col", [P, 2], fp32)
        tanh_g = sb("tanh_g", [P, 2], fp32)
        rate_g = sb("rate_g", [P, 1], fp32)
        eps_col = sb("eps_col", [P, 1], fp32)
        lqk_col = sb("lqk_col", [P, 1], fp32)
        gate_bias = sb("gate_bias", [2 * NH, 2], fp32)
        gw_raw = sb("gw_raw", [P, 3 * DC, 2 * NH], fp32)
        gw_sum = sb("gw_sum", [P, 2 * DC, 2 * NH], fp32)
        gw_hi = sb("gw_hi", [P, 2 * DC, 2 * NH], bf16)
        gw_lo = sb("gw_lo", [P, 2 * DC, 2 * NH], bf16)
        w_raw = sb("w_raw", [P, DC * F], fp32)
        wfc_hi = sb("wfc_hi", [P, DC, F], fp32r)
        wfc_lo = sb("wfc_lo", [P, DC, F], fp32r)
        wpr_hi = sb("wpr_hi", [P, FT, D], fp32r)
        wpr_lo = sb("wpr_lo", [P, FT, D], fp32r)

        x_in = [sb(f"x_in{i}", [P, ST, D], fp32) for i in range(NX)]
        v_in = [sb(f"v_in{i}", [P, ST, D], fp32) for i in range(NC)]
        kT_in = [sb(f"kT_in{i}", [P, DC, S], fp32) for i in range(NC)]
        stat1 = sb("stat1", [P, ST, 6], fp32)
        mv1 = [sb(f"mv1_{i}", [P, ST, 2], fp32) for i in range(2)]
        rstd1 = [sb(f"rstd1_{i}", [P, ST], fp32) for i in range(2)]
        lnv1 = sb("lnv1", [P, ST], fp32)
        xln = sb("xln", [P, ST, D], fp32)
        qT_hi = [sb(f"qT_hi{i}", [P, DC, S], bf16) for i in range(NQ)]
        qT_lo = [sb(f"qT_lo{i}", [P, DC, S], bf16) for i in range(NQ)]
        kT_hi = [sb(f"kT_hi{i}", [P, DC, S], bf16) for i in range(NQ)]
        kT_lo = [sb(f"kT_lo{i}", [P, DC, S], bf16) for i in range(NQ)]
        q_stack = [sb(f"q_stack{i}", [P, HPC, DC, S], bf16) for i in range(NST)]
        k_stack = [sb(f"k_stack{i}", [P, HPC, DC, S], bf16) for i in range(NST)]
        v_hi = [sb(f"v_hi{i}", [P, ST, NH, VW], bf16) for i in range(NV)]
        v_lo = [sb(f"v_lo{i}", [P, ST, NH, DH], bf16) for i in range(NV)]

        R = 2 * NH
        gates = [sb(f"gates{i}", [P, 2, ST, R], fp32) for i in range(2)]
        f_neg = sb("f_neg", [R, S], fp32)
        i_pre = sb("i_pre", [R, S], fp32)
        f_log = sb("f_log", [R, S], fp32)
        cs = sb("cs", [R, S], fp32)
        am = sb("am", [R, 2, S], fp32)
        row_max = sb("row_max", [R, S], fp32)
        am_rest = sb("am_rest", [R, 2, S], fp32)
        am_part = sb("am_part", [R, 3, 2, S], bf16)
        a_rows = [sb(f"a_rows{i}", [P, NH, S], bf16) for i in range(NAM)]
        m_rows = [sb(f"m_rows{i}", [P, NH, S], bf16) for i in range(NAM)]
        floor = [sb(f"floor{i}", [P, ST, R], fp32) for i in range(3)]

        decay = [sb(f"decay{i}", [P, BANK], fp32) for i in range(NUN)]
        c_hi = [sb(f"c_hi{i}", [P, BANK], bf16) for i in range(NCH)]
        c_lo = [sb(f"c_lo{i}", [P, BANK], bf16) for i in range(NCH)]

        denom = sb("denom", [P, ST, NH], fp32)
        rdenom = sb("rdenom", [P, ST, NH], fp32)
        h_rows = sb("h_rows", [P, ST, D], fp32)
        stat2 = sb("stat2", [P, ST, 6], fp32)
        mv2 = sb("mv2", [P, ST, 2], fp32)
        lnv2 = sb("lnv2", [P, ST], fp32)
        rstd2 = sb("rstd2", [P, ST], fp32)
        rstd2g = sb("rstd2g", [P, ST], fp32)
        x1 = [sb(f"x1_{i}", [P, 2 * ST, D], fp32) for i in range(NX1)]
        stat3 = sb("stat3", [P, ST, 6], fp32)
        mv3 = sb("mv3", [P, ST, 2], fp32)
        lnv3 = sb("lnv3", [P, ST], fp32)
        rstd3 = sb("rstd3", [P, ST], fp32)
        x1ln = sb("x1ln", [P, ST, D], fp32)
        x2_hi = [sb(f"x2_hi{i}", [P, DC, PT], fp32r) for i in range(NX2)]
        x2_lo = [sb(f"x2_lo{i}", [P, DC, PT], fp32r) for i in range(NX2)]

        relu = [sb(f"relu{i}", [P, PT], fp32) for i in range(NRE)]
        h_hi = [sb(f"h_hi{i}", [P, PT], fp32r) for i in range(NHF)]
        h_lo = [sb(f"h_lo{i}", [P, PT], fp32r) for i in range(NHF)]
        y_sb = w_raw[:, 0:DC * PT].rearrange("p (t d) -> p t d", d=D)
        spikes = sb("spikes", [P, 2 * ST, D], bf16)
        out_sb = w_raw[:, DC * PT:2 * DC * PT].rearrange("p (t d) -> p t d", d=D)

        arg_ps = ps("arg_ps", [P, BANK])
        qk_ps = ps("qk_ps", [P, BANK])
        z_ps = ps("z_ps", [P, BANK])
        misc_ps = ps("misc_ps", [P, BANK])
        pv_ps = ps("pv_ps", [P, ST, BANK])
        y_ps = ps("y_ps", [P, 2 * ST, D])
        pv_heads = pv_ps[:, :, 0:NH * VW].rearrange("p t (h c) -> p t h c", c=VW)

        sems = {}

        def sem(name):
            if name not in sems:
                sems[name] = ctx.enter_context(nc.semaphore(name))
            return sems[name]

        def after(eng, stage, n):
            if n >= 0:
                eng.wait_ge(sem(stage), n + 1)

        def landed(eng, ring, slot, n, dmas):
            eng.wait_ge(sem(f"{ring}{slot}"), 16 * dmas * (n + 1))

        streams = {k: [] for k in ("sync", "scalar", "vector", "tensor", "gpsimd")}

        def at(engine, time, step, *args):
            streams[engine].append((round(time, 3), len(streams[engine]), step, args))

        def play(engine, eng):
            for _, _, step, args in sorted(streams[engine], key=lambda e: e[:2]):
                step(eng, *args)

        chains = {}

        def link(eng, which, ins):
            chains[which] = chains.get(which, 0) + 1
            ins.then_inc(sem(f"chain_{which}"), 1)
            eng.wait_ge(sem(f"chain_{which}"), chains[which])

        misc_users = []

        def misc_turn(eng, user):
            after(eng, "misc_free", misc_use(user) - 1)

        def setup_load_small(e):
            e.dma_start(g_col[:, :], g_both.partition_broadcast(P)).then_inc(sem("ld_g"), 16)
            for dst, src in ((gw_raw[:, :, :], gate_w.rearrange("(c p) g -> p c g", p=P)),
                             (gate_bias[:, :], gate_b),
                             (scale_row[:, :], ln_scale.partition_broadcast(P))):
                e.dma_start(dst, src).then_inc(sem("ld_small"), 16)
        SMALL_LOADS = 3 * 16

        def setup_load_wfc(e):
            e.dma_start(w_raw[:, :], w_fc_t.rearrange("(c p) f -> p c f", p=P)).then_inc(sem("ld_wfc"), 16)

        def setup_load_wproj(e):
            after(e, "wfc_ready", 3)
            e.dma_start(w_raw[:, :], w_proj_t.rearrange("(j p) d -> p j d", p=P)).then_inc(sem("ld_wpr"), 16)

        def setup_pool(e):
            e.memset(ident[:, :], 0.0).then_inc(sem("zeroed"), 1)
            e.memset(ident_b[:, :], 0.0).then_inc(sem("zeroed"), 1)
            e.memset(behind[:, :], 0.0).then_inc(sem("zeroed"), 1)
            for t in v_hi:
                last = e.memset(t[:, :, :, DH:VW], 1.0)
            last.then_inc(sem("zeroed"), 1)
            e.wait_ge(sem("zeroed"), 4)
            e.affine_select(out=behind[:, :], in_=behind[:, :], compare_op=ALU.is_ge, fill=MASKED, base=0,
                            pattern=[[1, P]], channel_multiplier=-1).then_inc(sem("ident_ready"), 1)
            for t in (ident, ident_b):
                e.affine_select(out=t[:, :], in_=t[:, :], compare_op=ALU.not_equal, fill=1.0, base=0,
                                pattern=[[-1, P]], channel_multiplier=1).then_inc(sem("ident_ready"), 1)

        def setup_rows(e, i):
            def pair_of(value):
                top = int(np.array([value], np.float32).view(np.uint32)[0]) >> 16
                return float(np.array([top << 16 | top], np.uint32).view(np.float32)[0])

            def flat(t):
                return t[:, :, :].rearrange("p h s -> p (h s)").bitcast(fp32)

            link(e, "gpsimd", e.memset(flat(m_rows[i]), 0.0))
            e.memset(flat(m_rows[i])[0:3, :], pair_of(1.0))
            e.memset(flat(a_rows[i]), pair_of(-1.0)).then_inc(sem("rows_ready"), 1)

        def setup_cols(e):
            e.memset(eps_col[:, :], LN_EPS)
            e.memset(lqk_col[:, :], LOG_QK_SCALE).then_inc(sem("cols_ready"), 1)

        def setup_gates(e):
            e.wait_ge(sem("ld_small"), SMALL_LOADS)
            e.tensor_copy(gw_sum[:, 0:DC, :], gw_raw[:, 0:DC, :])
            link(e, "vector", e.tensor_tensor(gw_sum[:, DC:, :], gw_raw[:, DC:2 * DC, :], gw_raw[:, 2 * DC:, :], ALU.add))
            link(e, "vector", e.tensor_copy(gw_hi[:, :, :], gw_sum[:, :, :]))
            e.tensor_tensor(gw_lo[:, :, :], gw_sum[:, :, :], gw_hi[:, :, :], ALU.subtract).then_inc(sem("gw_ready"), 1)
            after(e, "tanh_ready", 0)
            e.tensor_scalar(rate_g[:, :], tanh_g[:, 1:2], 1.0 / STEPS, None, ALU.mult)

        def split_weights(e, stage, load, hi, lo, n):
            e.wait_ge(sem(load), 16)
            if n % 2:
                after(e, stage, n - 1)
            half = DC * F // 2
            cols = slice(n // 2 * half, (n // 2 + 1) * half)
            src, hi, lo = (t.rearrange("p a b -> p (a b)")[:, cols] if len(t.shape) == 3 else t[:, cols]
                           for t in (w_raw[:, :], hi[:, :, :], lo[:, :, :]))
            if n % 2 == 0:
                ins = e.tensor_copy(hi, src)
            else:
                ins = e.tensor_tensor(lo, src, hi.bitcast(fp32), ALU.subtract)
            ins.then_inc(sem(stage), 1)

        def setup_tanh(e):
            e.wait_ge(sem("ld_g"), 16)
            e.activation(tanh_g[:, :], g_col[:, :], ACT.Tanh).then_inc(sem("tanh_ready"), 1)
            e.preload_act_table_set("natural_log_exp_and_others")

        def load_batch(e, b):
            after(e, "x1_done", b - NX)
            e.dma_start(x_in[b % NX][:, :, :], x[b].rearrange("(t p) d -> p t d", p=P)).then_inc(sem(f"ld_x{b % NX}"), 16)
            after(e, "k_split", b - NC)
            e.dma_start(kT_in[b % NC][:, :, :], ctx_cols[b]).then_inc(sem(f"ld_k{b % NC}"), 16)

        def load_values(e, b):
            after(e, "v_split", b - NC)
            e.dma_start(v_in[b % NC][:, :, :], ctx_rows[b].rearrange("(t p) d -> p t d", p=P)).then_inc(sem(f"ld_v{b % NC}"), 16)

        def row_stats(e, src, stat, mv):
            for t in range(ST):
                ins = e.bn_stats(stat[:, t, :], src[:, t, :])
            link(e, "vector", ins)
            for t in range(ST):
                ins = e.bn_aggr(mv[:, t, :], stat[:, t, :])
            return ins

        def rstd_of(e, rstd, lnv, mv):
            link(e, "scalar", e.activation(lnv[:, :], mv[:, :, 1], ACT.Ln, bias=eps_col[:, :]))
            return e.activation(rstd[:, :], lnv[:, :], ACT.Exp, scale=-0.5)

        def normalise(e, dst, src, mv, rstd):
            for t in range(ST):
                ins = e.tensor_scalar(dst[:, t, :], src[:, t, :], mv[:, t, 0:1], rstd[:, t:t + 1], ALU.subtract, ALU.mult)
            return ins

        def ln1_stats(e, b):
            landed(e, "ld_x", b % NX, b // NX, 1)
            after(e, "xln", b - 2)
            row_stats(e, x_in[b % NX], stat1, mv1[b % 2]).then_inc(sem("ln1_stats"), 1)

        def ln1_rstd(e, b):
            after(e, "cols_ready", 0)
            after(e, "ln1_stats", b)
            after(e, "xln", b - 2)
            rstd_of(e, rstd1[b % 2], lnv1, mv1[b % 2]).then_inc(sem("ln1_rstd"), 1)

        def ln1_apply(e, b):
            after(e, "ln1_rstd", b)
            after(e, "q_T", b - 1)
            for t in range(ST):
                ins = e.tensor_scalar(xln[:, t, :].rearrange("p (c d g) -> p c g d", c=DC, g=HPC),
                                      x_in[b % NX][:, t, :].rearrange("p (c g d) -> p c g d", c=DC, g=HPC),
                                      mv1[b % 2][:, t, 0:1], rstd1[b % 2][:, t:t + 1], ALU.subtract, ALU.mult)
            ins.then_inc(sem("xln"), 1)

        def cast(e, step, dst, src):
            if ON[step] == "scalar":
                return e.activation(dst, src, ACT.Copy)
            if ON[step] == "vector":
                return e.tensor_copy(dst, src)
            return e.tensor_scalar(dst, src, 1.0, 1.0, ALU.mult, ALU.mult)

        def k_hi(e, b):
            landed(e, "ld_k", b % NC, b // NC, 1)
            after(e, "gates", b - NQ)
            if b >= NQ:
                landed(e, "ld_stack", (b - NQ) % NST, (b - NQ) // NST, STACK_DMAS)
            cast(e, "k_hi", kT_hi[b % NQ][:, :, :], kT_in[b % NC][:, :, :]).then_inc(sem("k_hi"), 1)

        def k_lo(e, b):
            after(e, "k_hi", b)
            e.tensor_tensor(kT_lo[b % NQ][:, :, :], kT_in[b % NC][:, :, :], kT_hi[b % NQ][:, :, :],
                            ALU.subtract).then_inc(sem("k_split"), 1)

        def v_heads(b):
            return v_in[b % NC][:, :, :].rearrange("p t (h d) -> p t h d", d=DH), v_hi[b % NV][:, :, :, 0:DH]

        def v_hi_step(e, b):
            landed(e, "ld_v", b % NC, b // NC, 1)
            after(e, "pv", 2 * (b - NV) + 1)
            src, hi = v_heads(b)
            cast(e, "v_hi", hi, src).then_inc(sem("v_hi"), 1)

        def v_lo_step(e, b):
            after(e, "v_hi", b)
            src, hi = v_heads(b)
            e.tensor_tensor(v_lo[b % NV][:, :, :, :], src, hi, ALU.subtract).then_inc(sem("v_split"), 1)

        def transpose_rows(e, src):
            for c in range(DC):
                for t in range(ST):
                    col = c * S + t * P
                    ins = e.transpose(misc_ps[:, col:col + P], src[:, t, c * P:(c + 1) * P], ident[:, :])
            return ins

        def q_T(e, b):
            e.wait_ge(sem("ident_ready"), 3)
            after(e, "xln", b)
            misc_turn(e, ("q", b))
            transpose_rows(e, xln).then_inc(sem("q_T"), 1)

        def misc_chunks():
            return misc_ps[:, :].rearrange("p (c s) -> p c s", c=DC)

        def q_hi(e, b):
            after(e, "q_T", b)
            after(e, "gates", b - NQ)
            if b >= NQ:
                landed(e, "ld_stack", (b - NQ) % NST, (b - NQ) // NST, STACK_DMAS)
            cast(e, "q_hi", qT_hi[b % NQ][:, :, :], misc_chunks()).then_inc(sem("q_hi"), 1)

        def q_lo(e, b):
            after(e, "q_hi", b)
            e.tensor_tensor(qT_lo[b % NQ][:, :, :], misc_chunks(), qT_hi[b % NQ][:, :, :],
                            ALU.subtract).then_inc(sem("misc_free"), 1)

        def misc_use(user):
            return [u for _, _, u in sorted(misc_users)].index(user)

        STACK_Q = ((0, qT_hi), (2, qT_hi), (1, qT_lo), (3, qT_lo))
        STACK_K = ((0, kT_hi), (1, kT_hi), (2, kT_lo), (3, kT_lo))
        STACK_DMAS = len(STACK_Q) + len(STACK_K)

        def stack_heads(e, b):
            slot = b % NST
            done = sem(f"ld_stack{slot}")
            after(e, "k_split", b)
            after(e, "misc_free", misc_use(("q", b)))
            after(e, "cmul", U * (b - NST) + U - 1)
            for stack, parts in ((k_stack, STACK_K), (q_stack, STACK_Q)):
                for j, part in parts:
                    dst = stack[slot][DH * j:DH * (j + 1), :, :, :].rearrange("d g c s -> d g (c s)")
                    e.dma_start(dst, part[b % NQ][:, :, :].rearrange("p c s -> p (c s)")).then_inc(done, 16)

        def gate_products(e, b):
            after(e, "gw_ready", 0)
            after(e, "k_split", b)
            after(e, "misc_free", misc_use(("q", b)))
            misc_turn(e, ("g", b))
            n = b % NQ
            for t in range(ST):
                terms = [(part[n][:, c, t * P:(t + 1) * P], w[:, k * DC + c, :])
                         for k, (hi, lo) in enumerate(((qT_hi, qT_lo), (kT_hi, kT_lo)))
                         for c in range(DC)
                         for part, w in ((hi, gw_hi), (hi, gw_lo), (lo, gw_hi))]
                for i, (lhsT, rhs) in enumerate(terms):
                    ins = e.matmul(misc_ps[:, t * R:(t + 1) * R], lhsT, rhs, start=(i == 0), stop=(i == len(terms) - 1))
            ins.then_inc(sem("gates"), 1)

        def gates_out(e, b):
            after(e, "gates", b)
            after(e, "gate_T", b // 2 - 2)
            src = misc_ps[:, 0:ST * R].rearrange("p (t k h) -> p k t h", t=ST, k=2)
            cast(e, "gates_out", gates[b // 2 % 2][:, :, :, b % 2 * NH:(b % 2 + 1) * NH], src).then_inc(sem("misc_free"), 1)

        def gate_T(e, p):
            after(e, "misc_free", misc_use(("g", 2 * p + 1)))
            misc_turn(e, ("gT", p))
            for k in range(2):
                for t in range(ST):
                    col = k * S + t * P
                    ins = e.transpose(misc_ps[0:R, col:col + P], gates[p % 2][:, k, t, :], ident[:, :])
            ins.then_inc(sem("gate_T"), 1)

        def gate_softplus(e, p):
            after(e, "gate_T", p)
            after(e, "gate_cummax", p - 1)
            ins = e.activation(f_log[:, :], misc_ps[0:R, S:2 * S], ACT.Abs, bias=gate_bias[:, 1:2])
            ins.then_inc(sem("gate_abs"), 1)
            after(e, "gate_abs", p)
            link(e, "scalar", e.activation(f_log[:, :], f_log[:, :], ACT.Exp, scale=-1.0))
            e.activation(f_log[:, :], f_log[:, :], ACT.Ln, bias=1.0).then_inc(sem("gate_softplus"), 1)

        def gate_pre(e, p):
            after(e, "gate_abs", p)
            e.tensor_scalar(f_neg[:, :], misc_ps[0:R, S:2 * S], gate_bias[:, 1:2], 0.0, ALU.add, ALU.min)
            e.tensor_scalar(i_pre[:, :], misc_ps[0:R, 0:S], gate_bias[:, 0:1], None, ALU.add).then_inc(sem("misc_free"), 1)

        def gate_cumsum(e, p):
            after(e, "gate_softplus", p)
            after(e, "misc_free", misc_use(("gT", p)))
            after(e, "am_split", 4 * p - 1)
            link(e, "vector", e.tensor_tensor_scan(cs[:, :], f_neg[:, :], f_log[:, :], 0.0, ALU.add, ALU.subtract))
            e.tensor_tensor(am[:, 0, :], i_pre[:, :], cs[:, :], ALU.subtract).then_inc(sem("gate_cumsum"), 1)

        def gate_cummax(e, p):
            after(e, "gate_cumsum", p)
            after(e, "floor_T", p - 1)
            a, m = am[:, 0, :], am[:, 1, :]
            link(e, "vector", e.tensor_tensor_scan(m, a, a, -3.0e38, ALU.max, ALU.max))
            e.tensor_tensor(row_max[:, :], m, cs[:, :], ALU.add).then_inc(sem("gate_cummax"), 1)

        def am_split(e, p, n):
            if n == 0:
                after(e, "gate_cummax", p)
                for b in (2 * p - 2, 2 * p - 1):
                    if b >= 0:
                        landed(e, "ld_am", b % NAM, b // NAM, AM_DMAS)
            else:
                after(e, "am_split", 4 * p + n - 1)
            src = am if n < 2 else am_rest
            hi = am_part[:, n // 2, :, :]
            if n % 2 == 0:
                ins = cast(e, "am_cast", hi, src[:, :, :])
            else:
                ins = e.tensor_tensor(am_rest[:, :, :] if n == 1 else am_part[:, 2, :, :], src[:, :, :], hi, ALU.subtract)
            ins.then_inc(sem("am_split"), 1)

        AM_DMAS = 6

        def am_rows(e, b):
            after(e, "rows_ready", min(b, NAM - 1))
            after(e, "am_split", 4 * (b // 2) + 3)
            after(e, "arg", U * (b - NAM + 1) - 1)
            mine = slice(b % 2 * NH, (b % 2 + 1) * NH)
            for k, (rows, first) in enumerate(((a_rows, 0), (m_rows, 3))):
                for j in range(3):
                    e.dma_start(rows[b % NAM][first + j:first + j + 1, :, :], am_part[mine, j, k, :])\
                     .then_inc(sem(f"ld_am{b % NAM}"), 16)

        def floor_T(e, p):
            after(e, "gate_cummax", p)
            misc_turn(e, ("fT", p))
            for t in range(ST):
                ins = e.transpose(misc_ps[:, t * R:(t + 1) * R], row_max[:, t * P:(t + 1) * P], ident[0:R, 0:R])
            ins.then_inc(sem("floor_T"), 1)

        def floor_exp(e, p):
            after(e, "floor_T", p)
            after(e, "h_norm", 2 * (p - 3) + 1)
            e.activation(floor[p % 3][:, :, :], misc_ps[:, 0:ST * R].rearrange("p (t r) -> p t r", t=ST), ACT.Exp,
                         scale=-1.0).then_inc(sem("misc_free"), 1)

        def unit_spans(kt, heads):
            n = S - kt * P
            return [(h, slice(i * n, (i + 1) * n), kt * P) for i, h in enumerate(heads)]

        def arg(e, b, u):
            kt, heads = UNITS[u]
            landed(e, "ld_am", b % NAM, b // NAM, AM_DMAS)
            after(e, "decay", b * U + u - 1)
            for h, cols, s0 in unit_spans(kt, heads):
                e.matmul(arg_ps[:, cols], a_rows[b % NAM][:, h, kt * P:(kt + 1) * P], m_rows[b % NAM][:, h, s0:S],
                         start=True, stop=False)
                ins = e.matmul(arg_ps[:, cols.start:cols.start + P], ident_b[:, :], behind[:, :], start=False, stop=True)
            ins.then_inc(sem("arg"), 1)

        def qk(e, b, u):
            kt, heads = UNITS[u]
            slot = b % NST
            landed(e, "ld_stack", slot, b // NST, STACK_DMAS)
            after(e, "cmul", b * U + u - 1)
            for h, cols, s0 in unit_spans(kt, heads):
                c, g = h // HPC, h % HPC
                ins = e.matmul(qk_ps[:, cols], k_stack[slot][:, g, c, kt * P:(kt + 1) * P], q_stack[slot][:, g, c, s0:S],
                               start=True, stop=True)
            ins.then_inc(sem("qk"), 1)

        def decay_exp(e, b, u):
            i = b * U + u
            after(e, "arg", i)
            after(e, "c_lo", i - NUN)
            e.activation(decay[i % NUN][:, :], arg_ps[:, :], ACT.Exp, bias=lqk_col[:, :]).then_inc(sem("decay"), 1)

        def cmul(e, b, u):
            i = b * U + u
            after(e, "qk", i)
            after(e, "decay", i)
            e.tensor_tensor(decay[i % NUN][:, :], qk_ps[:, :], decay[i % NUN][:, :], ALU.mult).then_inc(sem("cmul"), 1)

        def c_hi_step(e, b, u):
            i = b * U + u
            after(e, "cmul", i)
            after(e, "pv", (i - NCH) // 3)
            e.activation(c_hi[i % NCH][:, :], decay[i % NUN][:, :], ACT.Copy).then_inc(sem("c_hi"), 1)

        def c_lo_step(e, b, u):
            i = b * U + u
            after(e, "c_hi", i)
            e.tensor_tensor(c_lo[i % NCH][:, :], decay[i % NUN][:, :], c_hi[i % NCH][:, :], ALU.subtract).then_inc(sem("c_lo"), 1)

        def pv(e, b, half):
            first = half * 3
            after(e, "c_lo", b * U + first + 2)
            after(e, "v_split", b)
            if half == 0:
                after(e, "h_norm", b - 1)
            for qt in range(ST):
                for h in range(half * NH // 2, (half + 1) * NH // 2):
                    blocks = []
                    for u in range(first, first + 3):
                        kt, heads = UNITS[u]
                        if h in heads and kt <= qt:
                            col = heads.index(h) * (S - kt * P) + (qt - kt) * P
                            blocks.append((kt, (b * U + u) % NCH, col))
                    out_cols = pv_ps[:, qt, h * VW:(h + 1) * VW]
                    for n, (kt, slot, col) in enumerate(blocks):
                        hi, lo = c_hi[slot][:, col:col + P], c_lo[slot][:, col:col + P]
                        vh, vl = v_hi[b % NV][:, kt, h, :], v_lo[b % NV][:, kt, h, :]
                        e.matmul(out_cols, hi, vh, start=(n == 0), stop=False, skip_group_check=True)
                        e.matmul(pv_ps[:, qt, h * VW:h * VW + DH], hi, vl, start=False, stop=False, skip_group_check=True)
                        ins = e.matmul(out_cols, lo, vh, start=False, stop=(n == len(blocks) - 1), skip_group_check=True)
            ins.then_inc(sem("pv"), 1)

        def h_norm(e, b):
            p = b // 2
            after(e, "pv", 2 * b + 1)
            after(e, "misc_free", misc_use(("fT", p)))
            row_sum, least = pv_heads[:, :, :, DH], floor[p % 3][:, :, b % 2 * NH:(b % 2 + 1) * NH]
            link(e, "vector", e.scalar_tensor_tensor(denom[:, :, :], row_sum, -1.0, least, ALU.mult, ALU.max))
            link(e, "vector", e.tensor_tensor(denom[:, :, :], denom[:, :, :], row_sum, ALU.max))
            link(e, "vector", e.tensor_scalar(denom[:, :, :], denom[:, :, :], EPS, None, ALU.add))
            link(e, "vector", e.reciprocal(rdenom[:, :, :], denom[:, :, :]))
            heads = h_rows[:, :, :].rearrange("p t (h d) -> p t h d", d=DH)
            ins = e.tensor_tensor(heads, pv_heads[:, :, :, 0:DH],
                                  rdenom[:, :, :].unsqueeze(3).broadcast_to([P, ST, NH, DH]), ALU.mult)
            ins.then_inc(sem("h_norm"), 1)

        def ln2_stats(e, b):
            after(e, "h_norm", b)
            row_stats(e, h_rows, stat2, mv2).then_inc(sem("ln2_stats"), 1)

        def ln2_rstd(e, b):
            after(e, "ln2_stats", b)
            after(e, "x1_done", b - 1)
            rstd_of(e, rstd2, lnv2, mv2).then_inc(sem("ln2_rstd"), 1)

        def x1_step(e, b):
            after(e, "tanh_ready", 0)
            after(e, "ln2_rstd", b)
            after(e, "out_done", b // 2 - NX1)
            for t in range(ST):
                e.scalar_tensor_tensor(h_rows[:, t, :], h_rows[:, t, :], mv2[:, t, 0:1], scale_row[:, :],
                                       ALU.subtract, ALU.mult)
            link(e, "vector", e.tensor_scalar(rstd2g[:, :], rstd2[:, :], tanh_g[:, 0:1], None, ALU.mult))
            dst = x1[b // 2 % NX1][:, b % 2 * ST:(b % 2 + 1) * ST, :]
            for t in range(ST):
                ins = e.scalar_tensor_tensor(dst[:, t, :], h_rows[:, t, :], rstd2g[:, t:t + 1], x_in[b % NX][:, t, :],
                                             ALU.mult, ALU.add)
            ins.then_inc(sem("x1_done"), 1)

        def ln3_stats(e, b):
            after(e, "x1_done", b)
            after(e, "x1ln", b - 1)
            row_stats(e, x1[b // 2 % NX1][:, b % 2 * ST:(b % 2 + 1) * ST, :], stat3, mv3).then_inc(sem("ln3_stats"), 1)

        def ln3_rstd(e, b):
            after(e, "ln3_stats", b)
            after(e, "x1ln", b - 1)
            rstd_of(e, rstd3, lnv3, mv3).then_inc(sem("ln3_rstd"), 1)

        def ln3_apply(e, b):
            after(e, "ln3_rstd", b)
            after(e, "x2_T", b - 1)
            normalise(e, x1ln, x1[b // 2 % NX1][:, b % 2 * ST:(b % 2 + 1) * ST, :], mv3, rstd3).then_inc(sem("x1ln"), 1)

        def x2_T(e, b):
            after(e, "x1ln", b)
            misc_turn(e, ("x2", b))
            transpose_rows(e, x1ln).then_inc(sem("x2_T"), 1)

        def x2_cols(tiles, b):
            return tiles[b // 2 % NX2][:, :, b % 2 * S:(b % 2 + 1) * S]

        def x2_hi_step(e, b):
            after(e, "x2_T", b)
            after(e, "z", FT * (b // 2 - NX2 + 1) - 1)
            cast(e, "x2_hi", x2_cols(x2_hi, b), misc_chunks()).then_inc(sem("x2_hi"), 1)

        def x2_lo_step(e, b):
            after(e, "x2_hi", b)
            e.tensor_tensor(x2_cols(x2_lo, b), misc_chunks(), x2_cols(x2_hi, b).bitcast(fp32),
                            ALU.subtract).then_inc(sem("misc_free"), 1)

        JOBS = [(p, slice(0, 2 * ST)) for p in range(PAIRS - 1)] + [(PAIRS - 1, slice(0, ST)), (PAIRS - 1, slice(ST, 2 * ST))]

        def job_before(q):
            return q - 1 if q < PAIRS else PAIRS - 2

        def tokens(q):
            tiles = JOBS[q][1]
            return slice(tiles.start * P, tiles.stop * P)

        def z_step(e, q, j):
            p, tiles = JOBS[q]
            if j == 0:
                after(e, "wfc_ready", 3)
                after(e, "misc_free", misc_use(("x2", 2 * p + tiles.stop // ST - 1)))
            after(e, "relu", FT * q + j - 1)
            xh, xl = x2_hi[p % NX2], x2_lo[p % NX2]
            terms = [(w[:, c, j * P:(j + 1) * P], xx[:, c, tokens(q)]) for c in range(DC)
                     for w, xx in ((wfc_hi, xh), (wfc_hi, xl), (wfc_lo, xh))]
            for n, (lhsT, rhs) in enumerate(terms):
                ins = e.matmul(z_ps[:, tokens(q)], lhsT, rhs, start=(n == 0), stop=(n == len(terms) - 1))
            ins.then_inc(sem("z"), 1)

        def relu_step(e, q, j):
            n = FT * q + j
            after(e, "z", n)
            after(e, "h_lo", n - NRE)
            e.activation(relu[n % NRE][:, tokens(q)], z_ps[:, tokens(q)], ACT.Relu).then_inc(sem("relu"), 1)

        def h_full_step(e, q, j):
            n = FT * q + j
            after(e, "relu", n)
            r = relu[n % NRE][:, tokens(q)]
            if j in SQUARES_ON_ACT:
                e.activation(r, r, ACT.Square).then_inc(sem("square_act"), 1)
            else:
                e.tensor_tensor(r, r, r, ALU.mult).then_inc(sem("square_dve"), 1)

        def after_square(e, q, j):
            on_act = [j2 in SQUARES_ON_ACT for j2 in range(FT)]
            mine = [j2 for j2 in range(FT) if on_act[j2] == on_act[j]]
            after(e, "square_act" if on_act[j] else "square_dve", len(mine) * q + mine.index(j))

        def h_hi_step(e, q, j):
            n = FT * q + j
            after_square(e, q, j)
            after(e, "y", n - NHF)
            e.activation(h_hi[n % NHF][:, tokens(q)], relu[n % NRE][:, tokens(q)], ACT.Copy).then_inc(sem("h_hi"), 1)

        def h_lo_step(e, q, j):
            n = FT * q + j
            after(e, "h_hi", n)
            e.tensor_tensor(h_lo[n % NHF][:, tokens(q)], relu[n % NRE][:, tokens(q)],
                            h_hi[n % NHF][:, tokens(q)].bitcast(fp32), ALU.subtract).then_inc(sem("h_lo"), 1)

        def y_step(e, q, j):
            n = FT * q + j
            if j == 0:
                after(e, "wpr_ready", 3)
                after(e, "y_out", job_before(q))
            after(e, "h_lo", n)
            hh, hl = h_hi[n % NHF], h_lo[n % NHF]
            for t in range(JOBS[q][1].start, JOBS[q][1].stop):
                terms = [(h[:, t * P:(t + 1) * P], w[:, j, :]) for w, h in ((wpr_hi, hh), (wpr_lo, hh), (wpr_hi, hl))]
                for i, (lhsT, rhs) in enumerate(terms):
                    ins = e.matmul(y_ps[:, t, :], lhsT, rhs, start=(j == 0 and i == 0 and t % ST == 0),
                                   stop=(j == FT - 1 and i == len(terms) - 1), skip_group_check=True)
            ins.then_inc(sem("y"), 1)

        def y_out(e, q):
            tiles = JOBS[q][1]
            after(e, "y", FT * q + FT - 1)
            after(e, "spikes", STEPS * (job_before(q) + 1) - 1)
            cast(e, "y_out", y_sb[:, tiles, :], y_ps[:, tiles, :]).then_inc(sem("y_out"), 1)

        def spikes_step(e, q, n):
            y, count = y_sb[:, JOBS[q][1], :], spikes[:, JOBS[q][1], :]
            if n == 0:
                after(e, "y_out", q)
                after(e, "out_done", job_before(q))
                ins = e.tensor_scalar(count, y, THETA[0], None, ALU.is_gt)
            else:
                after(e, "spikes", STEPS * q + n - 1)
                ins = e.scalar_tensor_tensor(count, y, THETA[n], count, ALU.is_gt, ALU.add)
            ins.then_inc(sem("spikes"), 1)

        def out_step(e, q):
            p, tiles = JOBS[q]
            after(e, "spikes", STEPS * (q + 1) - 1)
            if p >= 1:
                landed(e, "stored", 0, p - 1, 2)
            e.scalar_tensor_tensor(out_sb[:, tiles, :], spikes[:, tiles, :], rate_g[:, :], x1[p % NX1][:, tiles, :],
                                   ALU.mult, ALU.add).then_inc(sem("out_done"), 1)

        def store(e, q):
            p, tiles = JOBS[q]
            after(e, "out_done", q)
            for b in range(tiles.start // ST, tiles.stop // ST):
                e.dma_start(out[2 * p + b].rearrange("(t p) d -> p t d", p=P), out_sb[:, b * ST:(b + 1) * ST, :])\
                 .then_inc(sem("stored0"), 16)

        at("scalar", -1e3, setup_load_small)
        at("sync", PLAN["load_wfc"], setup_load_wfc)
        at("sync", PLAN["load_wproj"], setup_load_wproj)
        at("gpsimd", -1e3, setup_pool)
        for i in range(NAM):
            at("gpsimd", PLAN[f"rows{i}"], setup_rows, i)
        at("vector", -1e3, setup_cols)
        at("vector", PLAN["setup_gates"], setup_gates)
        at("scalar", -1e3, setup_tanh)
        for n in range(4):
            at("vector", PLAN["split_wfc"] + n, split_weights, "wfc_ready", "ld_wfc", wfc_hi, wfc_lo, n)
            at("vector", PLAN["split_wproj"] + n, split_weights, "wpr_ready", "ld_wpr", wpr_hi, wpr_lo, n)

        def use_misc(time, step, user, *args):
            misc_users.append((round(time, 3), len(streams["tensor"]), user))
            at("tensor", time, step, *args)

        def times(base, k):
            return {name: base + (v if np.isscalar(v) else v[k % len(v)]) for name, v in PLAN.items()}

        for b in range(B):
            t0 = U * b
            t = times(t0, b % 2)
            at("sync", t["load"], load_batch, b)
            at("vector", t["ln1_stats"], ln1_stats, b)
            at("scalar", t["ln1_rstd"], ln1_rstd, b)
            at(ON["xln"], t["xln"], ln1_apply, b)
            at(ON["k_hi"], t["k_hi"], k_hi, b)
            at(ON["k_lo"], t["k_lo"], k_lo, b)
            at("sync", t["load_v"], load_values, b)
            at(ON["v_hi"], t["v_hi"], v_hi_step, b)
            at(ON["v_lo"], t["v_lo"], v_lo_step, b)
            use_misc(t["q_T"], q_T, ("q", b), b)
            at(ON["q_hi"], t["q_hi"], q_hi, b)
            at("vector", t["q_lo"], q_lo, b)
            at("sync", t["stack"], stack_heads, b)
            use_misc(t["gates"], gate_products, ("g", b), b)
            at(ON["gates_out"], t["gates_out"], gates_out, b)
            at("sync", t["am_rows"], am_rows, b)
            for u in range(U):
                t = times(t0 + u, b % 2 * U + u)
                at("tensor", t["arg"], arg, b, u)
                at("tensor", t["qk"], qk, b, u)
                at("scalar", t["decay"], decay_exp, b, u)
                at("vector", t["cmul"], cmul, b, u)
                at("scalar", t["c_hi"], c_hi_step, b, u)
                at("gpsimd", t["c_lo"], c_lo_step, b, u)
            t = times(t0, b % 2)
            for half in range(2):
                at("tensor", t[f"pv{half}"], pv, b, half)
            at("vector", t["h_norm"], h_norm, b)
            at("vector", t["ln2_stats"], ln2_stats, b)
            at("scalar", t["ln2_rstd"], ln2_rstd, b)
            at("vector", t["x1"], x1_step, b)
            at("vector", t["ln3_stats"], ln3_stats, b)
            at("scalar", t["ln3_rstd"], ln3_rstd, b)
            at(ON["x1ln"], t["x1ln"], ln3_apply, b)
            use_misc(t["x2_T"], x2_T, ("x2", b), b)
            at(ON["x2_hi"], t["x2_hi"], x2_hi_step, b)
            at("vector", t["x2_lo"], x2_lo_step, b)
        for p in range(PAIRS):
            t0 = 2 * U * p
            t = times(t0, 0)
            use_misc(t["gate_T"], gate_T, ("gT", p), p)
            at("scalar", t["gate_softplus"], gate_softplus, p)
            at("vector", t["gate_pre"], gate_pre, p)
            at("vector", t["gate_cumsum"], gate_cumsum, p)
            at("vector", t["gate_cummax"], gate_cummax, p)
            for n in range(4):
                at(ON["am_rest" if n % 2 else "am_cast"], t[f"am_split{n}"], am_split, p, n)
            use_misc(t["floor_T"], floor_T, ("fT", p), p)
            at("scalar", t["floor_exp"], floor_exp, p)
        for q, (p, _) in enumerate(JOBS):
            t0 = 2 * U * p
            if q >= PAIRS - 1:
                t0 = t0 + PLAN[f"half{q - (PAIRS - 1)}"]
            for j in range(FT):
                t = times(t0, j)
                at("tensor", t["z"], z_step, q, j)
                at("scalar", t["relu"], relu_step, q, j)
                at("scalar" if j in SQUARES_ON_ACT else "vector", t["h_full"], h_full_step, q, j)
                at("scalar", t["h_hi"], h_hi_step, q, j)
                at("gpsimd", t["h_lo"], h_lo_step, q, j)
                at("tensor", t["y"], y_step, q, j)
            t = times(t0, 0)
            at(ON["y_out"], t["y_out"], y_out, q)
            for n in range(STEPS):
                at("vector", times(t0, n)["spikes"], spikes_step, q, n)
            at("vector", t["out"], out_step, q)
            at("sync", t["store"], store, q)

        block = ctx.enter_context(nc.Block())

        @block.sync
        def _(eng):
            play("sync", eng)
            landed(eng, "stored", 0, PAIRS - 1, 2)

        @block.scalar
        def _(eng):
            play("scalar", eng)

        @block.vector
        def _(eng):
            play("vector", eng)

        @block.tensor
        def _(eng):
            play("tensor", eng)

        @block.gpsimd
        def _(eng):
            play("gpsimd", eng)


def kernel(x, ctx_1024, g_xattn, g_ffn, L0_xattn_igate_w, L0_xattn_igate_b, L0_xattn_fgate_w, L0_xattn_fgate_b,
           L0_xattn_ln_scale, L0_ffn_W_fc, L0_ffn_W_proj):
    import concourse.bacc as bacc
    from concourse.bass_utils import run_bass_kernel_spmd

    nh, d = L0_xattn_igate_w.shape[0], x.shape[2]
    dh, p = d // nh, 128

    def head_minor(a):
        return a.reshape(-1, p // dh, dh, a.shape[-1]).transpose(0, 2, 1, 3).reshape(a.shape)

    ctx_t = np.transpose(ctx_1024, (0, 2, 1))
    cols = head_minor(ctx_t.reshape(-1, ctx_t.shape[-1])).reshape(ctx_t.shape[0], d // p, p, -1)
    arrays = {
        "x": x,
        "ctx_rows": ctx_1024,
        "ctx_cols": np.transpose(cols, (0, 2, 1, 3)),
        "g_both": np.stack([g_xattn.reshape(()), g_ffn.reshape(())]),
        "gate_w": head_minor(np.transpose(np.concatenate([L0_xattn_igate_w, L0_xattn_fgate_w], axis=0))),
        "gate_b": np.tile(np.stack([L0_xattn_igate_b, L0_xattn_fgate_b], axis=1), (2, 1)),
        "ln_scale": L0_xattn_ln_scale,
        "w_fc_t": np.transpose(L0_ffn_W_fc),
        "w_proj_t": np.transpose(L0_ffn_W_proj),
    }
    arrays = {n: np.ascontiguousarray(a) for n, a in arrays.items()}
    nc = bacc.Bacc("TRN2", target_bir_lowering=False, num_devices=1)
    args = [nc.dram_tensor(n, a.shape, mybir.dt.from_np(a.dtype), kind="ExternalInput").ap() for n, a in arrays.items()]
    out = nc.dram_tensor("out", x.shape, mybir.dt.float32, kind="ExternalOutput").ap()
    build_block(nc, *args, out)
    r = run_bass_kernel_spmd(nc, [arrays], core_ids=[0])
    return r.results[0]["out"]
```
